# Optimizing a Trainium2 kernel written in Bass

```python
import numpy as np
import jax
import jax.numpy as jnp

def _softmax(x, axis=-1):
    return jax.nn.softmax(x, axis=axis)

def _gelu(x):
    return jax.nn.gelu(x, approximate=True)

def _silu(x):
    return jax.nn.silu(x)

def _sigmoid(x):
    return jax.nn.sigmoid(x)

def _layernorm(x, axis=-1, eps=1e-05):
    m = jnp.mean(x, axis=axis, keepdims=True)
    v = jnp.var(x, axis=axis, keepdims=True)
    return (x - m) / jnp.sqrt(v + eps)

def _scatter_add(tgt, idx, src, axis=0):
    return tgt.at[idx].add(src)

def _segment_sum(src, seg, n):
    return jax.ops.segment_sum(src, seg, n)
kernel_name = 'mk_xattn_ffn_d1_seqx_r8_06e3af'

def setup_inputs(seed: int=0):
    np.random.seed(seed)
    _w = jnp.asarray

    def _rec_inputs():
        import jax
        import jax.numpy as jnp
        _rk = jax.random.key(seed)
        x = -7.109e-05 + 0.9999 * jax.random.normal(jax.random.fold_in(_rk, 1), (16, 64, 512), jnp.float32)
        _lenS = 64 - jax.random.randint(jax.random.fold_in(_rk, 7), (16,), 0, max(1, 64 // 4) + 1, jnp.int32)
        _lenS2 = 64 - jax.random.randint(jax.random.fold_in(_rk, 8), (16,), 0, max(1, 64 // 4) + 1, jnp.int32)
        _ctx_4096P = jax.random.normal(jax.random.fold_in(_rk, 11), (16, 16, 512), jnp.float32)
        _ctx_4096c = jax.random.dirichlet(jax.random.fold_in(_rk, 511), 0.3 * jnp.ones((16,), jnp.float32), (16, 64))
        _ctx_4096t = jnp.einsum('bsk,bkd->bsd', _ctx_4096c, _ctx_4096P)
        _ctx_4096t = _ctx_4096t * jax.lax.rsqrt(jnp.mean(jnp.square(_ctx_4096t)) + 1e-12) * 0.953939
        ctx_4096 = -2.6191e-05 + 0.999952 * (_ctx_4096t + 0.3 * jax.random.normal(jax.random.fold_in(_rk, 611), (16, 64, 512), jnp.float32))
        return (x, ctx_4096)
    x, ctx_4096 = _rec_inputs()

    def _L0_xattn_setup():
        import jax, jax.numpy as jnp
        import numpy as np
        TEXT_DIM = 512
        FEATURE_DIM = 512

        def _xavier_uniform(key, shape):
            fan_in, fan_out = (shape[1], shape[0])
            limit = float(np.sqrt(6.0 / (fan_in + fan_out)))
            return jax.random.uniform(key, shape, jnp.float32, -limit, limit)
        key = jax.random.key(seed)
        k1, k2, k3, k4 = jax.random.split(key, 4)
        text = jax.random.normal(k1, (8, 256, TEXT_DIM), jnp.float32)
        features = jax.random.normal(k2, (8, 72, FEATURE_DIM), jnp.float32)
        Wq = _xavier_uniform(k3, (FEATURE_DIM, TEXT_DIM))
        bq = jnp.zeros((FEATURE_DIM,), jnp.float32)
        Wk = _xavier_uniform(k4, (FEATURE_DIM, FEATURE_DIM))
        bk = jnp.zeros((FEATURE_DIM,), jnp.float32)
        return {'text': text, 'features': features, 'Wq': Wq, 'bq': bq, 'Wk': Wk, 'bk': bk}
    _L0_xattn_all = _L0_xattn_setup()
    _L0_xattn_in = {k: v for k, v in _L0_xattn_all.items() if k in ('Wq', 'bq', 'Wk', 'bk')}
    del _L0_xattn_all

    def _L0_ffn_setup():
        import jax, jax.numpy as jnp
        import numpy as np
        HIDDEN = 512
        MOE_INTER = 128
        SHARED_INTER = 512
        NUM_EXPERTS = 16
        TOP_K = 2

        def _moe_forward(x, gate_w, w_gate_up, w_down, shared_w_gate_up, shared_w_down):
            orig_shape = x.shape
            x2 = x.reshape(-1, orig_shape[-1])
            gu_s = x2 @ shared_w_gate_up.T
            g_s, u_s = jnp.split(gu_s, 2, axis=-1)
            shared_out = jax.nn.silu(g_s) * u_s @ shared_w_down.T
            logits = x2 @ gate_w.T
            probs = jax.nn.softmax(logits, axis=-1)
            topk_vals, topk_idx = jax.lax.top_k(probs, TOP_K)
            topk_vals = topk_vals / jnp.sum(topk_vals, axis=-1, keepdims=True)
            combine = jnp.sum(jax.nn.one_hot(topk_idx, NUM_EXPERTS, dtype=x2.dtype) * topk_vals[..., None], axis=1)
            gu = jnp.einsum('th,eih->eti', x2, w_gate_up)
            g, u = jnp.split(gu, 2, axis=-1)
            act = jax.nn.silu(g) * u
            out_e = jnp.einsum('eti,ehi->eth', act, w_down)
            moe_out = jnp.einsum('eth,te->th', out_e, combine)
            return (moe_out + shared_out).reshape(orig_shape)
        key = jax.random.key(seed)
        ks = jax.random.split(key, 6)
        s = 0.02
        hidden_states = jax.random.normal(ks[0], (2, 256, HIDDEN), dtype=jnp.float32)
        gate_w = jax.random.normal(ks[1], (NUM_EXPERTS, HIDDEN), dtype=jnp.float32) * s
        w_gate_up = jax.random.normal(ks[2], (NUM_EXPERTS, 2 * MOE_INTER, HIDDEN), dtype=jnp.float32) * s
        w_down = jax.random.normal(ks[3], (NUM_EXPERTS, HIDDEN, MOE_INTER), dtype=jnp.float32) * s
        shared_w_gate_up = jax.random.normal(ks[4], (2 * SHARED_INTER, HIDDEN), dtype=jnp.float32) * s
        shared_w_down = jax.random.normal(ks[5], (HIDDEN, SHARED_INTER), dtype=jnp.float32) * s
        return {'hidden_states': hidden_states, 'gate_w': gate_w, 'w_gate_up': w_gate_up, 'w_down': w_down, 'shared_w_gate_up': shared_w_gate_up, 'shared_w_down': shared_w_down}
    _L0_ffn_all = _L0_ffn_setup()
    _L0_ffn_in = {k: v for k, v in _L0_ffn_all.items() if k in ('gate_w', 'w_gate_up', 'w_down', 'shared_w_gate_up', 'shared_w_down')}
    del _L0_ffn_all
    return {'x': x, 'ctx_4096': ctx_4096, 'L0_xattn_Wq': _L0_xattn_in['Wq'], 'L0_xattn_bq': _L0_xattn_in['bq'], 'L0_xattn_Wk': _L0_xattn_in['Wk'], 'L0_xattn_bk': _L0_xattn_in['bk'], 'L0_ffn_gate_w': _L0_ffn_in['gate_w'], 'L0_ffn_w_gate_up': _L0_ffn_in['w_gate_up'], 'L0_ffn_w_down': _L0_ffn_in['w_down'], 'L0_ffn_shared_w_gate_up': _L0_ffn_in['shared_w_gate_up'], 'L0_ffn_shared_w_down': _L0_ffn_in['shared_w_down']}

def reference(x, ctx_4096, L0_xattn_Wq, L0_xattn_bq, L0_xattn_Wk, L0_xattn_bk, L0_ffn_gate_w, L0_ffn_w_gate_up, L0_ffn_w_down, L0_ffn_shared_w_gate_up, L0_ffn_shared_w_down):
    import jax
    import jax.numpy as jnp

    def _L0_xattn_ref(text, features, Wq, bq, Wk, bk):
        import jax, jax.numpy as jnp
        import numpy as np
        TEXT_DIM = 512
        FEATURE_DIM = 512

        def _xavier_uniform(key, shape):
            fan_in, fan_out = (shape[1], shape[0])
            limit = float(np.sqrt(6.0 / (fan_in + fan_out)))
            return jax.random.uniform(key, shape, jnp.float32, -limit, limit)
        Q = jnp.einsum('btx,dx->btd', text, Wq) + bq
        K = jnp.einsum('bpx,dx->bpd', features, Wk) + bk
        scale = 1.0 / jnp.sqrt(jnp.asarray(K.shape[-1], K.dtype))
        scores = jnp.einsum('btd,bpd->btp', Q, K) * scale
        attn = jax.nn.softmax(scores, axis=-1)
        attended = jnp.einsum('btp,bpd->btd', attn, features)
        return attended

    def _L0_ffn_ref(hidden_states, gate_w, w_gate_up, w_down, shared_w_gate_up, shared_w_down):
        import jax, jax.numpy as jnp
        import numpy as np
        HIDDEN = 512
        MOE_INTER = 128
        SHARED_INTER = 512
        NUM_EXPERTS = 16
        TOP_K = 2

        def _moe_forward(x, gate_w, w_gate_up, w_down, shared_w_gate_up, shared_w_down):
            orig_shape = x.shape
            x2 = x.reshape(-1, orig_shape[-1])
            gu_s = x2 @ shared_w_gate_up.T
            g_s, u_s = jnp.split(gu_s, 2, axis=-1)
            shared_out = jax.nn.silu(g_s) * u_s @ shared_w_down.T
            logits = x2 @ gate_w.T
            probs = jax.nn.softmax(logits, axis=-1)
            topk_vals, topk_idx = jax.lax.top_k(probs, TOP_K)
            topk_vals = topk_vals / jnp.sum(topk_vals, axis=-1, keepdims=True)
            combine = jnp.sum(jax.nn.one_hot(topk_idx, NUM_EXPERTS, dtype=x2.dtype) * topk_vals[..., None], axis=1)
            gu = jnp.einsum('th,eih->eti', x2, w_gate_up)
            g, u = jnp.split(gu, 2, axis=-1)
            act = jax.nn.silu(g) * u
            out_e = jnp.einsum('eti,ehi->eth', act, w_down)
            moe_out = jnp.einsum('eth,te->th', out_e, combine)
            return (moe_out + shared_out).reshape(orig_shape)
        return _moe_forward(hidden_states, gate_w, w_gate_up, w_down, shared_w_gate_up, shared_w_down)
    x = x + _L0_xattn_ref(_layernorm(x, axis=-1), ctx_4096, L0_xattn_Wq, L0_xattn_bq, L0_xattn_Wk, L0_xattn_bk)
    x = x + _L0_ffn_ref(_layernorm(x, axis=-1), L0_ffn_gate_w, L0_ffn_w_gate_up, L0_ffn_w_down, L0_ffn_shared_w_gate_up, L0_ffn_shared_w_down)
    return x

_drawn_inputs = setup_inputs


def setup_inputs(seed=0):
    import zlib

    import numpy as np

    out = dict(_drawn_inputs(seed))
    spreads = {'L0_xattn_bq': (0.0, 0.41), 'L0_xattn_bk': (0.0, 0.8)}
    factors = {'L0_ffn_gate_w': 4.0, 'L0_ffn_w_gate_up': 3.684, 'L0_ffn_w_down': 3.703}
    for name, (base, spread) in spreads.items():
        noise = np.random.default_rng([zlib.crc32(name.encode()), seed]).standard_normal(out[name].shape)
        drawn = base * np.exp(spread * noise) if base else spread * noise
        out[name] = jnp.asarray(drawn.astype(out[name].dtype))
    for name, factor in factors.items():
        out[name] = (out[name] * factor).astype(out[name].dtype)
    return out
```

```python
from contextlib import ExitStack

import concourse.bass as bass
from concourse import mybir

F32 = mybir.dt.float32
I32 = mybir.dt.int32
U32 = mybir.dt.uint32
ALU = mybir.AluOpType
ACT = mybir.ActivationFunctionType
AX = mybir.AxisListType

P = 128


def xattn_moe(nc, x, ctx_t, ctx_n, wq_t, wk_t, bq, bk, gate_t, moe_gu_t, moe_dn_t, sh_gu_t, sh_dn_t, out):
    _, NT, D = x.shape
    T = NT * P
    C = D // P
    SEQ = 64
    NE = gate_t.shape[2]
    TOPK = 2
    FE = moe_dn_t.shape[0]
    SC = sh_dn_t.shape[1]
    HALF = NT // 2
    HW = HALF * P
    NS = T * TOPK // P + NE - 1
    SCALE = float(D) ** -0.5
    EPS = 1e-5

    xn_dram = nc.dram_tensor("xn_dram", (T, D), F32, kind="Internal").ap()
    y_dram = nc.dram_tensor("y_dram", (NS * P, D), F32, kind="Internal").ap()

    with ExitStack() as ctx:
        def sb(name, shape, dt=F32):
            return ctx.enter_context(nc.sbuf_tensor(name, shape, dt))

        def sem(name):
            return ctx.enter_context(nc.semaphore(name))

        bank = [ctx.enter_context(nc.psum_tensor(f"bank{i}", [P, 512], F32)) for i in range(8)]

        GUW = C * 2 * FE
        moe_gu = sb("moe_gu", [P, NE * GUW])
        moe_dn = sb("moe_dn", [P, NE * D])
        ctxT = moe_gu[:, 0:4096].rearrange("p (c t) -> p c t", c=C)
        ctxN = moe_gu[:, 4096:8192].rearrange("p (t d) -> p t d", t=NT)
        wqT = moe_gu[:, 8192:10240].rearrange("p (c o) -> p c o", c=C)
        wkT = moe_gu[:, 10240:12288].rearrange("p (c o) -> p c o", c=C)
        kT = moe_gu[:, 12288:16384].rearrange("p (c t) -> p c t", c=C)
        qT = moe_dn[:, 4096:8192].rearrange("p (c t) -> p c t", c=C)
        sh_gu = sb("sh_gu", [P, C, 2 * SC * P])
        sh_dn = sb("sh_dn", [P, SC, D])
        xs = sb("xs", [P, NT, D])
        xn = sb("xn", [P, NT, D])
        xnT = sb("xnT", [P, C, T])
        hsT = sb("hsT", [P, SC, HW])
        gate = sb("gate", [P, C, NE])
        bqs = sb("bqs", [P, C])
        bks = sb("bks", [P, C])
        ident = sb("ident", [P, P])
        before = sb("before", [P, P])
        ones = sb("ones", [P, P])
        iota_f = sb("iota_f", [P, P])
        tokid = sb("tokid", [P, NT])
        steps128 = sb("steps128", [P, 8])
        lower_e = sb("lower_e", [P, NE, NE])
        neg_half = sb("neg_half", [P, 2 * NT])
        stats = sb("stats", [P, NT, 6])
        meanvar = sb("meanvar", [P, NT, 2])
        vareps = sb("vareps", [P, NT])
        rstd = sb("rstd", [P, NT])
        E = [hsT[:, h, :].rearrange("p (t k) -> p t k", t=HALF) for h in range(2)]
        ET = hsT[:, 2, :].rearrange("p (t k) -> p t k", t=HALF)
        smax = sb("smax", [P, NT])
        ssum = sb("ssum", [P, NT])
        rsum = sb("rsum", [P, NT])
        silu_s = [sb(f"silu_s{i}", [P, HW]) for i in range(2)]
        rmax = sb("rmax", [P, NT])
        prob = sb("prob", [P, NT, NE])
        psm = sb("psm", [P, NT])
        prs = sb("prs", [P, NT])
        top = sb("top", [P, NT, 8])
        topi = sb("topi", [P, NT, 8], U32)
        topf = sb("topf", [P, NT, TOPK])
        wsum = sb("wsum", [P, NT])
        wrec = sb("wrec", [P, NT])
        wtop = sb("wtop", [P, NT, TOPK])
        pick = [sb(f"pick{k}", [P, NT, NE]) for k in range(TOPK)]
        picked = sb("picked", [P, NT, NE])
        over = sb("over", [P, NE, 8])
        ntile = sb("ntile", [P, NE])
        prod_e = sb("prod_e", [P, NE, NE])
        first = sb("first", [P, NE])
        place = sb("place", [P, NT, NE])
        placed = [sb(f"placed{k}", [P, NT, NE]) for k in range(TOPK)]
        rows = sb("rows", [P, NT, TOPK])
        rows_i = sb("rows_i", [P, NT, TOPK], I32)
        rows_u = sb("rows_u", [P, NT, TOPK], U32)
        slot_i = sb("slot_i", [P, NT, TOPK], I32)
        slot_f = sb("slot_f", [P, NT, TOPK])
        inrow = sb("inrow", [P, NT, TOPK])
        last_e = sb("last_e", [1, NE])
        past = sb("past", [1, 32, NE])
        slot_e = sb("slot_e", [1, 32])
        slot_exp = sb("slot_exp", [1, 32], I32)
        rowhot = [sb(f"rowhot{i}", [P, P]) for i in range(4)]
        slothot = sb("slothot", [P, NT * TOPK, 32])
        src_rows = sb("src_rows", [P, 32], U32)
        NG = 4
        grow = [sb(f"grow{i}", [P, D]) for i in range(NG)]
        gT = [silu_s[i][:].rearrange("p (c t) -> p c t", c=C) for i in range(2)]
        sg = [sb(f"sg{i}", [P, FE]) for i in range(2)]
        hh = [sb(f"hh{i}", [P, FE]) for i in range(2)]
        hT = [sb(f"hT{i}", [P, P]) for i in range(2)]
        ys = [hsT[:, i, :] for i in range(2)]

        ld = {n: sem(f"ld_{n}") for n in ("small", "wk", "ctxT0", "ctxT1", "x0", "x1", "wq", "ctxN", "shgu", "shdn",
                                          "dn0", "dn1", "gu0", "gu1", "gu2", "gu3")}
        const_step = sem("const_step")
        const_ready = sem("const_ready")
        dve_step = sem("dve_step")
        zeroed = sem("zeroed")
        var_ready = sem("var_ready")
        rstd_ready = sem("rstd_ready")
        xn_ready = sem("xn_ready")
        xn_stored = sem("xn_stored")
        proj_done = sem("proj_done")
        proj_out = sem("proj_out")
        ring_done = sem("ring_done")
        ring_out = sem("ring_out")
        score_done = sem("score_done")
        shifted = sem("shifted")
        exp_done = sem("exp_done")
        exp_half = sem("exp_half")
        shift_half = sem("shift_half")
        et_done = sem("et_done")
        et_out = sem("et_out")
        logit_done = sem("logit_done")
        rshift = sem("rshift")
        rexp = sem("rexp")
        pair_done = sem("pair_done")
        pair_silu = sem("pair_silu")
        pair_out = sem("pair_out")
        picked_ready = sem("picked_ready")
        count_done = sem("count_done")
        exp_table = sem("exp_table")
        slothot_ready = sem("slothot_ready")
        rowhot_ready = sem("rowhot_ready")
        rowhot_used = sem("rowhot_used")
        src_ready = sem("src_ready")
        rows_ready = sem("rows_ready")
        gathered = [sem(f"gathered{i}") for i in range(NG)]
        turned = sem("turned")
        gT_out = sem("gT_out")
        gu_done = sem("gu_done")
        silu_done = sem("silu_done")
        h_ready = sem("h_ready")
        h_turned = sem("h_turned")
        hT_out = sem("hT_out")
        y_done = sem("y_done")
        y_out = sem("y_out")
        y_stored = [sem(f"y_stored{i}") for i in range(2)]
        back = [sem(f"back{i}") for i in range(NG)]
        back_used = sem("back_used")
        fin_step = sem("fin_step")
        fin_ready = sem("fin_ready")
        stored = sem("stored")

        LOOP0 = 3
        LOOPN = (NS - 1 - LOOP0) // NG

        def slot_steps(eng, step):
            for s in range(LOOP0):
                step(s, s)
            with eng.Fori(0, LOOPN) as i:
                for u in range(NG):
                    step(NG * i + (LOOP0 + u), LOOP0 + u)
            for s in range(LOOP0 + NG * LOOPN, NS):
                step(s, s)

        def ge(eng, s, value):
            if not isinstance(value, int) or value > 0:
                eng.wait_ge(s, value)

        def is_first(s, n):
            return isinstance(s, int) and s < n

        block = ctx.enter_context(nc.Block())

        @block.sync
        def _(sp):
            def load(name, dst, src):
                sp.dma_start(dst, src).then_inc(ld[name], 16)

            load("wk", wkT, wk_t)
            load("ctxT0", ctxT[:, :, 0:HW], ctx_t[:, :, 0:HW])
            load("x0", xs[:, 0:HALF, :], x[:, 0:HALF, :])
            load("small", bqs[:], bq)
            load("small", bks[:], bk)
            load("small", gate[:], gate_t)
            load("ctxT1", ctxT[:, :, HW:T], ctx_t[:, :, HW:T])
            load("wq", wqT, wq_t)
            load("x1", xs[:, HALF:NT, :], x[:, HALF:NT, :])
            load("ctxN", ctxN, ctx_n)
            load("shgu", sh_gu[:], sh_gu_t)
            load("shdn", sh_dn[:], sh_dn_t)
            load("dn0", moe_dn[:, 0:4096], moe_dn_t.rearrange("p e d -> p (e d)")[:, 0:4096])
            gu_flat = moe_gu_t.rearrange("p e c i -> p (e c i)")
            sp.wait_ge(proj_done, 16)
            load("gu0", moe_gu[:, 0:4096], gu_flat[:, 0:4096])
            load("gu1", moe_gu[:, 8192:12288], gu_flat[:, 8192:12288])
            sp.wait_ge(score_done, 2)
            load("gu2", moe_gu[:, 12288:16384], gu_flat[:, 12288:16384])
            load("dn1", moe_dn[:, 4096:8192], moe_dn_t.rearrange("p e d -> p (e d)")[:, 4096:8192])
            sp.wait_ge(ring_done, 16)
            load("gu3", moe_gu[:, 4096:8192], gu_flat[:, 4096:8192])
            for h in range(2):
                sp.wait_ge(xn_ready, NT + HALF * (h + 1))
                sp.dma_start(xn_dram[h * HW:(h + 1) * HW, :].rearrange("(t p) d -> p t d", p=P),
                             xn[:, h * HALF:(h + 1) * HALF, :]).then_inc(xn_stored, 16)

            def store(s, m):
                sp.wait_ge(y_out, s + 1)
                dst = y_dram[bass.ds(s * P, P), :] if not isinstance(s, int) else y_dram[s * P:(s + 1) * P, :]
                sp.dma_start(dst, ys[m % 2]).then_inc(y_stored[m % 2], 16)

            slot_steps(sp, store)
            for t in range(NT):
                sp.wait_ge(fin_ready, t + 1)
                sp.dma_start(out[:, t, :], xs[:, t, :]).then_inc(stored, 16)
            sp.wait_ge(stored, 16 * NT)

        @block.gpsimd
        def _(pool):
            steps = [0]

            def then(ins):
                steps[0] += 1
                ins.then_inc(const_step, 1)
                pool.wait_ge(const_step, steps[0])

            nc.gpsimd.memset(neg_half[:], -0.5).then_inc(const_ready, 1)
            then(nc.gpsimd.memset(ident[:], 0.0))
            nc.gpsimd.affine_select(out=ident[:], in_=ident[:], compare_op=ALU.not_equal, fill=1.0, base=0,
                                    pattern=[[-1, P]], channel_multiplier=1).then_inc(const_ready, 1)
            for h in range(2):
                then(nc.gpsimd.memset(E[h], 0.0))
            nc.gpsimd.memset(ones[:], 1.0).then_inc(const_ready, 1)

            def rsqrt(n, a, b):
                pool.wait_ge(var_ready, n)
                nc.gpsimd.tensor_tensor(out=rstd[:, a:b], in0=vareps[:, a:b], in1=neg_half[:, a:b],
                                        op=ALU.pow).then_inc(rstd_ready, 1)

            pool.wait_ge(const_ready, 3)
            rsqrt(1, 0, HALF)
            rsqrt(2, HALF, NT)
            then(nc.gpsimd.memset(before[:], 1.0))
            nc.gpsimd.affine_select(out=before[:], in_=before[:], compare_op=ALU.is_gt, fill=0.0, base=0,
                                    pattern=[[1, P]], channel_multiplier=-1).then_inc(const_ready, 1)
            nc.gpsimd.iota(iota_f[:], pattern=[[1, P]], base=0, channel_multiplier=0,
                           allow_small_or_imprecise_dtypes=True).then_inc(const_ready, 1)
            nc.gpsimd.iota(tokid[:], pattern=[[P, NT]], base=0, channel_multiplier=1,
                           allow_small_or_imprecise_dtypes=True).then_inc(const_ready, 1)
            nc.gpsimd.iota(steps128[:], pattern=[[P, 8]], base=0, channel_multiplier=0,
                           allow_small_or_imprecise_dtypes=True).then_inc(const_ready, 1)
            then(nc.gpsimd.memset(lower_e[:], 1.0))
            nc.gpsimd.affine_select(out=lower_e[:], in_=lower_e[:], compare_op=ALU.is_gt, fill=0.0, base=0,
                                    pattern=[[1, NE], [-1, NE]], channel_multiplier=0).then_inc(const_ready, 1)
            rsqrt(3, 0, HALF)
            rsqrt(4, HALF, NT)
            pool.wait_ge(src_ready, 1)
            pool.wait_ge(xn_stored, 32)
            for s in range(NS):
                ge(pool, turned, s - NG + 1)
                nc.gpsimd.indirect_dma_start(
                    out=grow[s % NG][:], out_offset=None, in_=xn_dram,
                    in_offset=bass.IndirectOffsetOnAxis(ap=src_rows[:, s:s + 1], axis=0),
                ).then_inc(gathered[s % NG], 16)
            pool.wait_ge(turned, NS)
            pool.wait_ge(y_stored[0], 16 * ((NS + 1) // 2))
            pool.wait_ge(y_stored[1], 16 * (NS // 2))
            pool.wait_ge(rows_ready, 1)
            for n in range(NT * TOPK):
                t, k = n // TOPK, n % TOPK
                ge(pool, back_used, n - NG + 1)
                nc.gpsimd.indirect_dma_start(
                    out=grow[n % NG][:], out_offset=None, in_=y_dram,
                    in_offset=bass.IndirectOffsetOnAxis(ap=rows_u[:, t, k:k + 1], axis=0),
                ).then_inc(back[n % NG], 16)

        @block.tensor
        def _(pe):
            def mm(o, w, m, start, stop):
                return nc.tensor.matmul(o, w, m, start=start, stop=stop)

            def project(n, w, mov, h):
                for o in range(C):
                    if n + o >= 4:
                        pe.wait_ge(proj_out, n + o - 3)
                    for c in range(C):
                        last = mm(bank[(n + o) % 4][:], w[:, c, o * P:(o + 1) * P], mov[:, c, h * HW:(h + 1) * HW],
                                  c == 0, c == C - 1)
                    last.then_inc(proj_done, 1)

            def ring(m):
                if m >= 2:
                    pe.wait_ge(ring_out, m - 1)
                return bank[4 + m % 2]

            def turn_xn(m, h, xn_before):
                for j in range(HALF):
                    t = h * HALF + j
                    pe.wait_ge(xn_ready, xn_before + t + 1)
                    b = ring(m + j)
                    for c in range(C):
                        last = nc.tensor.transpose(b[:, c * P:(c + 1) * P], xn[:, t, c * P:(c + 1) * P], ident[:])
                    last.then_inc(ring_done, 1)

            def scores(h):
                pe.wait_ge(proj_out, 12 + 4 * h)
                if h:
                    pe.wait_ge(shifted, 1)
                for j in range(HALF):
                    a = (h * HALF + j) * P
                    for c in range(C):
                        last = mm(bank[6][:, j * P:(j + 1) * P], qT[:, c, a:a + P], kT[:, c, a:a + P],
                                  c == 0, c == C - 1)
                last.then_inc(score_done, 1)

            def turn_exp(h):
                pe.wait_ge(exp_done, h + 1)
                if h:
                    pe.wait_ge(et_out, 1)
                for j in range(HALF):
                    last = nc.tensor.transpose(bank[7][:, j * P:(j + 1) * P], E[h][:, j, :], ident[:])
                last.then_inc(et_done, 1)

            def attend(m, h):
                pe.wait_ge(et_out, h + 1)
                pe.wait_ge(ld["ctxN"], 16)
                for j in range(HALF):
                    b = ring(m + j)
                    mm(b[:], ET[:, j, :], ctxN[:, h * HALF + j, :], True, True).then_inc(ring_done, 1)

            def shared_pair(h, j):
                n = h * SC + j
                if n >= 2:
                    pe.wait_ge(pair_out, n - 1)
                if n == 0:
                    pe.wait_ge(ld["shgu"], 16)
                for g in range(2):
                    for c in range(C):
                        a = g * SC * P + j * P
                        last = mm(bank[2 * (n % 2) + g][:], sh_gu[:, c, a:a + P], xnT[:, c, h * HW:(h + 1) * HW],
                                  c == 0, c == C - 1)
                last.then_inc(pair_done, 1)

            def shared_down(m, h):
                pe.wait_ge(pair_out, (h + 1) * SC)
                pe.wait_ge(ld["shdn"], 16)
                for j in range(HALF):
                    b = ring(m + j)
                    for c in range(SC):
                        last = mm(b[:], hsT[:, c, j * P:(j + 1) * P], sh_dn[:, c, :], c == 0, c == SC - 1)
                    last.then_inc(ring_done, 1)

            pe.wait_ge(ld["wk"], 16)
            pe.wait_ge(ld["ctxT0"], 16)
            project(0, wkT, ctxT, 0)
            pe.wait_ge(ld["ctxT1"], 16)
            project(4, wkT, ctxT, 1)
            pe.wait_ge(const_ready, 2)
            turn_xn(0, 0, 0)
            pe.wait_ge(ld["wq"], 16)
            pe.wait_ge(ring_out, 4)
            project(8, wqT, xnT, 0)
            scores(0)
            turn_xn(4, 1, 0)
            pe.wait_ge(ring_out, 8)
            project(12, wqT, xnT, 1)
            turn_exp(0)
            scores(1)
            attend(8, 0)
            turn_exp(1)
            attend(12, 1)
            turn_xn(16, 0, NT)
            pe.wait_ge(ring_out, 20)
            pe.wait_ge(proj_out, 16)
            shared_pair(0, 0)
            turn_xn(20, 1, NT)
            pe.wait_ge(ring_out, 24)
            pe.wait_ge(ld["small"], 48)
            pe.wait_ge(shifted, 2)
            for t in range(NT):
                for c in range(C):
                    last = mm(bank[6][:, t * NE:(t + 1) * NE], xnT[:, c, t * P:(t + 1) * P], gate[:, c, :],
                              c == 0, c == C - 1)
            last.then_inc(logit_done, 1)
            shared_pair(0, 1)
            pe.wait_ge(picked_ready, 1)
            pe.wait_ge(const_ready, 8)
            W = NT * NE
            pk = picked[:].rearrange("p t e -> p (t e)")
            mm(bank[7][:, 0:W], before[:], pk, True, False)
            for d in range(1, NT):
                mm(bank[7][:, d * NE:W], ones[:], pk[:, 0:W - d * NE], False, d == NT - 1)
            for t in range(NT):
                last = mm(bank[6][:, 256:256 + NE], ones[:], picked[:, t, :], t == 0, t == NT - 1)
            last.then_inc(count_done, 1)
            shared_pair(0, 2)
            shared_pair(0, 3)
            pe.wait_ge(slothot_ready, 1)
            for n in range(NT * TOPK):
                pe.wait_ge(rowhot_ready, n + 1)
                mm(bank[7][:, 256:288], rowhot[n % 4][:], slothot[:, n, :], n == 0,
                   n == NT * TOPK - 1).then_inc(rowhot_used, 1)
            shared_down(24, 0)

            pe.wait_ge(exp_table, 1)
            for n in ("dn0", "dn1", "gu0", "gu1", "gu2", "gu3"):
                pe.wait_ge(ld[n], 16)

            def expert_of(s):
                src = slot_exp[0:1, s:s + 1] if isinstance(s, int) else slot_exp[0:1, bass.ds(s, 1)]
                return pe.value_load(src, min_val=0, max_val=NE - 1)

            def turn(s, m):
                g = m % NG
                pe.wait_ge(gathered[g], 16 * ((s - g) // NG + 1) if isinstance(s, int) else loop_turn(s, m))
                ge(pe, gT_out, s - 1)
                b = bank[4 + m % 2]
                for c in range(C):
                    last = nc.tensor.transpose(b[:, c * P:(c + 1) * P], grow[g][:, c * P:(c + 1) * P], ident[:])
                last.then_inc(turned, 1)

            def gate_up(s, m, e, chunks):
                if 0 in chunks:
                    pe.wait_ge(gT_out, s + 1)
                    ge(pe, h_ready, s - 1)
                for c in chunks:
                    last = mm(bank[m % 2][:, 0:2 * FE], gT[m % 2][:, c, :],
                              moe_gu[:, bass.ds(e * GUW + c * 2 * FE, 2 * FE)], c == 0, c == C - 1)
                if C - 1 in chunks:
                    last.then_inc(gu_done, 1)

            def turn_h(s, m):
                pe.wait_ge(h_ready, s + 1)
                ge(pe, hT_out, s - 1)
                nc.tensor.transpose(bank[2 + m % 2][:, 0:P], hh[m % 2][:], ident[:]).then_inc(h_turned, 1)

            def down(s, m, e):
                pe.wait_ge(hT_out, s + 1)
                ge(pe, y_out, s - 1)
                mm(bank[6 + m % 2][:], hT[m % 2][:], moe_dn[:, bass.ds(e * D, D)], True, True).then_inc(y_done, 1)

            counter = [None]

            def loop_turn(s, m):
                return 16 * counter[0] + 16 * (m // NG + 1)

            def step(s, m):
                more = not (isinstance(s, int) and s + 1 >= NS)
                if more:
                    turn(s + 1, m + 1)
                e = expert_of(s)
                gate_up(s, m, e, (0, 1))
                if m:
                    turn_h(s - 1, m - 1)
                gate_up(s, m, e, (2, 3))
                if m:
                    down(s - 1, m - 1, expert_of(s - 1))

            pe.wait_ge(ring_out, 28)
            pe.wait_ge(src_ready, 1)
            turn(0, 0)
            for s in range(LOOP0):
                step(s, s)
            with pe.Fori(0, LOOPN) as i:
                counter[0] = i
                for u in range(NG):
                    step(NG * i + (LOOP0 + u), LOOP0 + u)
            for s in range(LOOP0 + NG * LOOPN, NS):
                step(s, s)
            turn_h(NS - 1, NS - 1)
            down(NS - 1, NS - 1, expert_of(NS - 1))

            pe.wait_ge(h_ready, NS)
            pe.wait_ge(hT_out, NS)
            for j in range(SC):
                shared_pair(1, j)
            shared_down(28, 1)

        @block.scalar
        def _(act):
            act.wait_ge(ld["small"], 48)

            def proj_evac(n, dst, bias, h):
                for o in range(C):
                    act.wait_ge(proj_done, n + o + 1)
                    nc.scalar.activation(dst[:, o, h * HW:(h + 1) * HW], bank[(n + o) % 4][:], ACT.Identity,
                                         bias=bias[:, o:o + 1]).then_inc(proj_out, 1)

            def softmax_exp(h):
                act.wait_ge(shifted, h + 1)
                for b in range(2):
                    r = slice(b * SEQ, (b + 1) * SEQ)
                    last = nc.scalar.activation(E[h][r, :, r], E[h][r, :, r], ACT.Exp, scale=SCALE)
                    if b == 0:
                        last.then_inc(exp_half, 1)
                last.then_inc(exp_done, 1)

            def et_evac(h):
                act.wait_ge(et_done, h + 1)
                if h:
                    act.wait_ge(ring_done, 12)
                nc.scalar.copy(ET, bank[7][:].rearrange("p (t k) -> p t k", t=HALF)).then_inc(et_out, 1)

            def pair_silu_step(n):
                act.wait_ge(pair_done, n + 1)
                if n >= 2:
                    act.wait_ge(pair_out, n - 1)
                nc.scalar.activation(silu_s[n % 2][:], bank[2 * (n % 2)][:], ACT.Silu).then_inc(pair_silu, 1)

            proj_evac(0, kT, bks, 0)
            proj_evac(4, kT, bks, 1)
            proj_evac(8, qT, bqs, 0)
            softmax_exp(0)
            proj_evac(12, qT, bqs, 1)
            et_evac(0)
            softmax_exp(1)
            et_evac(1)
            pair_silu_step(0)
            act.wait_ge(rshift, 1)
            nc.scalar.activation(prob[:], prob[:], ACT.Exp).then_inc(rexp, 1)
            for n in range(1, SC):
                pair_silu_step(n)

            def evac_gT(s, m):
                act.wait_ge(turned, s + 1)
                ge(act, gu_done, s - 1)
                nc.scalar.copy(gT[m % 2], bank[4 + m % 2][:].rearrange("p (c t) -> p c t", c=C)).then_inc(gT_out, 1)

            def step(s, m):
                if not (isinstance(s, int) and s + 1 >= NS):
                    evac_gT(s + 1, m + 1)
                act.wait_ge(gu_done, s + 1)
                ge(act, h_ready, s - 1)
                nc.scalar.activation(sg[m % 2][:], bank[m % 2][:, 0:FE], ACT.Silu).then_inc(silu_done, 1)

            act.wait_ge(pair_out, SC)
            evac_gT(0, 0)
            slot_steps(act, step)
            for n in range(SC, 2 * SC):
                pair_silu_step(n)


        @block.vector
        def _(dve):
            steps = [0]

            def then(ins):
                steps[0] += 1
                ins.then_inc(dve_step, 1)
                dve.wait_ge(dve_step, steps[0])

            def bn(t):
                then(nc.vector.bn_stats(stats[:, t, :], xs[:, t, :]))
                then(nc.vector.bn_aggr(meanvar[:, t, :], stats[:, t, :]))

            def var(h):
                a, b = h * HALF, (h + 1) * HALF
                nc.vector.tensor_scalar(vareps[:, a:b], meanvar[:, a:b, 1], EPS, None, ALU.add).then_inc(var_ready, 1)

            def normalise(n, h):
                dve.wait_ge(rstd_ready, n)
                for t in range(h * HALF, (h + 1) * HALF):
                    nc.vector.tensor_scalar(xn[:, t, :], xs[:, t, :], meanvar[:, t, 0:1], rstd[:, t:t + 1],
                                            ALU.subtract, ALU.mult).then_inc(xn_ready, 1)

            def xnT_evac(m, h):
                for j in range(HALF):
                    a = (h * HALF + j) * P
                    dve.wait_ge(ring_done, m + j + 1)
                    nc.vector.tensor_copy(xnT[:, :, a:a + P],
                                          bank[4 + (m + j) % 2][:].rearrange("p (c t) -> p c t", c=C))\
                        .then_inc(ring_out, 1)

            def softmax_shift(h):
                dve.wait_ge(score_done, h + 1)
                s = bank[6][:].rearrange("p (t k) -> p t k", t=HALF)
                mx = smax[:, h * HALF:(h + 1) * HALF]
                for b in range(2):
                    r = slice(b * SEQ, (b + 1) * SEQ)
                    then(nc.vector.tensor_reduce(mx[r, :], s[r, :, r], AX.X, ALU.max))
                for b in range(2):
                    r = slice(b * SEQ, (b + 1) * SEQ)
                    last = nc.vector.tensor_tensor(E[h][r, :, r], s[r, :, r],
                                                   mx[r, :].unsqueeze(2).to_broadcast([SEQ, HALF, SEQ]), ALU.subtract)
                    if b == 0:
                        last.then_inc(shift_half, 1)
                last.then_inc(shifted, 1)

            def softmax_sum(h):
                dve.wait_ge(exp_done, h + 1)
                dve.wait_ge(exp_half, h + 1)
                a, b = h * HALF, (h + 1) * HALF
                then(nc.vector.tensor_reduce(ssum[:, a:b], E[h], AX.X, ALU.add))
                then(nc.vector.reciprocal(rsum[:, a:b], ssum[:, a:b]))

            def residual(m, h):
                for j in range(HALF):
                    t = h * HALF + j
                    dve.wait_ge(ring_done, m + j + 1)
                    nc.vector.scalar_tensor_tensor(out=xs[:, t, :], in0=bank[4 + (m + j) % 2][:],
                                                   scalar=rsum[:, t:t + 1], in1=xs[:, t, :],
                                                   op0=ALU.mult, op1=ALU.add).then_inc(ring_out, 1)
                    dve.wait_ge(ring_out, m + j + 1)
                    bn(t)

            def pair_mul(n):
                dve.wait_ge(pair_silu, n + 1)
                if n == SC:
                    dve.wait_ge(ring_done, 28)
                    dve.wait_ge(y_stored[0], 16 * ((NS + 1) // 2))
                    dve.wait_ge(y_stored[1], 16 * (NS // 2))
                nc.vector.tensor_tensor(hsT[:, n % SC, :], bank[2 * (n % 2) + 1][:], silu_s[n % 2][:], ALU.mult)\
                    .then_inc(pair_out, 1)

            def add_shared(m, h):
                for j in range(HALF):
                    t = h * HALF + j
                    dve.wait_ge(ring_done, m + j + 1)
                    nc.vector.tensor_tensor(xs[:, t, :], bank[4 + (m + j) % 2][:], xs[:, t, :], ALU.add)\
                        .then_inc(ring_out, 1)

            dve.wait_ge(const_step, 3)
            for h in range(2):
                dve.wait_ge(ld[f"x{h}"], 16)
                for t in range(h * HALF, (h + 1) * HALF):
                    bn(t)
                var(h)
                if h == 0:
                    normalise(1, 0)
            normalise(2, 1)
            xnT_evac(0, 0)
            xnT_evac(4, 1)
            softmax_shift(0)
            softmax_sum(0)
            softmax_shift(1)
            residual(8, 0)
            var(0)
            softmax_sum(1)
            residual(12, 1)
            var(1)
            normalise(3, 0)
            normalise(4, 1)
            xnT_evac(16, 0)
            pair_mul(0)
            xnT_evac(20, 1)

            dve.wait_ge(logit_done, 1)
            dve.wait_ge(const_ready, 8)
            lg = bank[6][:, 0:NT * NE].rearrange("p (t e) -> p t e", t=NT)

            def over_e(ap):
                return ap.unsqueeze(2).to_broadcast([P, NT, NE])

            then(nc.vector.tensor_reduce(rmax[:], lg, AX.X, ALU.max))
            nc.vector.tensor_tensor(prob[:], lg, over_e(rmax[:]), ALU.subtract).then_inc(rshift, 1)
            dve.wait_ge(rexp, 1)
            then(nc.vector.tensor_reduce(psm[:], prob[:], AX.X, ALU.add))
            then(nc.vector.reciprocal(prs[:], psm[:]))
            then(nc.vector.tensor_tensor(prob[:], prob[:], over_e(prs[:]), ALU.mult))
            for t in range(NT):
                then(nc.vector.max(top[:, t, :], prob[:, t, :]))
            for t in range(NT):
                then(nc.vector.max_index(topi[:, t, :], top[:, t, :], prob[:, t, :]))
            then(nc.vector.tensor_copy(topf[:], topi[:, :, 0:TOPK]))
            it = iota_f[:, 0:NE].unsqueeze(1).to_broadcast([P, NT, NE])
            for k in range(TOPK):
                then(nc.vector.tensor_tensor(pick[k][:], it, over_e(topf[:, :, k]), ALU.is_equal))
            nc.vector.tensor_tensor(picked[:], pick[0][:], pick[1][:], ALU.add).then_inc(picked_ready, 1)
            then(nc.vector.tensor_tensor(wsum[:], top[:, :, 0], top[:, :, 1], ALU.add))
            then(nc.vector.reciprocal(wrec[:], wsum[:]))
            then(nc.vector.tensor_tensor(wtop[:], top[:, :, 0:TOPK], wrec[:].unsqueeze(2).to_broadcast([P, NT, TOPK]),
                                         ALU.mult))
            pair_mul(1)
            dve.wait_ge(count_done, 1)
            then(nc.vector.tensor_tensor(over[:], bank[6][:, 256:256 + NE].unsqueeze(2).to_broadcast([P, NE, 8]),
                                         steps128[:].unsqueeze(1).to_broadcast([P, NE, 8]), ALU.is_gt))
            then(nc.vector.tensor_reduce(ntile[:], over[:], AX.X, ALU.add))
            then(nc.vector.tensor_tensor(prod_e[:], lower_e[:], ntile[:].unsqueeze(1).to_broadcast([P, NE, NE]),
                                         ALU.mult))
            then(nc.vector.tensor_reduce(first[:], prod_e[:], AX.X, ALU.add))
            then(nc.vector.scalar_tensor_tensor(out=place[:], in0=first[:].unsqueeze(1).to_broadcast([P, NT, NE]),
                                                scalar=float(P),
                                                in1=bank[7][:, 0:NT * NE].rearrange("p (t e) -> p t e", t=NT),
                                                op0=ALU.mult, op1=ALU.add))
            for k in range(TOPK):
                then(nc.vector.tensor_tensor(placed[k][:], pick[k][:], place[:], ALU.mult))
            for k in range(TOPK):
                then(nc.vector.tensor_reduce(rows[:, :, k], placed[k][:], AX.X, ALU.add))
            then(nc.vector.tensor_copy(rows_i[:], rows[:]))
            nc.vector.tensor_copy(rows_u[:], rows[:]).then_inc(rows_ready, 1)
            then(nc.vector.tensor_scalar(slot_i[:], rows_i[:], 7, None, ALU.arith_shift_right))
            then(nc.vector.tensor_copy(slot_f[:], slot_i[:]))
            then(nc.vector.scalar_tensor_tensor(out=inrow[:], in0=slot_f[:], scalar=-float(P), in1=rows[:],
                                                op0=ALU.mult, op1=ALU.add))
            R = NT * TOPK
            sf = slot_f[:].rearrange("p t k -> p (t k)")
            ir = inrow[:].rearrange("p t k -> p (t k)")
            then(nc.vector.tensor_tensor(slothot[:], iota_f[:, 0:32].unsqueeze(1).to_broadcast([P, R, 32]),
                                         sf.unsqueeze(2).to_broadcast([P, R, 32]), ALU.is_equal))
            sh4 = slothot[:].rearrange("p (t k) s -> p t (k s)", k=TOPK)
            nc.vector.tensor_tensor(sh4, sh4, tokid[:].unsqueeze(2).to_broadcast([P, NT, TOPK * 32]), ALU.mult)\
                .then_inc(slothot_ready, 1)
            pair_mul(2)
            for n in range(R):
                if n >= 4:
                    dve.wait_ge(rowhot_used, n - 3)
                nc.vector.tensor_scalar(rowhot[n % 4][:], iota_f[:], ir[:, n:n + 1], None, ALU.is_equal)\
                    .then_inc(rowhot_ready, 1)
                if n == 3:
                    then(nc.vector.tensor_tensor(last_e[:], first[0:1, :], ntile[0:1, :], ALU.add))
                    then(nc.vector.tensor_tensor(past[:], last_e[:].unsqueeze(1).to_broadcast([1, 32, NE]),
                                                 iota_f[0:1, 0:32].unsqueeze(2).to_broadcast([1, 32, NE]), ALU.is_le))
                    then(nc.vector.tensor_reduce(slot_e[:], past[:], AX.X, ALU.add))
                    nc.vector.tensor_scalar(slot_exp[:], slot_e[:], float(NE - 1), None, ALU.min)\
                        .then_inc(exp_table, 1)
                    pair_mul(3)
            dve.wait_ge(rowhot_used, R)
            nc.vector.tensor_copy(src_rows[:], bank[7][:, 256:288]).then_inc(src_ready, 1)
            add_shared(24, 0)

            def out_h(s, m):
                dve.wait_ge(h_turned, s + 1)
                ge(dve, y_done, s - 1)
                nc.vector.tensor_copy(hT[m % 2][:], bank[2 + m % 2][:, 0:P]).then_inc(hT_out, 1)

            def mul_h(s, m):
                dve.wait_ge(silu_done, s + 1)
                ge(dve, h_turned, s - 1)
                nc.vector.tensor_tensor(hh[m % 2][:], bank[m % 2][:, FE:2 * FE], sg[m % 2][:], ALU.mult)\
                    .then_inc(h_ready, 1)

            counter = [None]

            def out_y(s, m):
                dve.wait_ge(y_done, s + 1)
                if isinstance(s, int):
                    ge(dve, y_stored[m % 2], 16 * (s // 2))
                else:
                    dve.wait_ge(y_stored[m % 2], 32 * counter[0] + 16 * (m // 2))
                nc.vector.tensor_copy(ys[m % 2], bank[6 + m % 2][:]).then_inc(y_out, 1)

            def step(s, m):
                if m:
                    out_h(s - 1, m - 1)
                mul_h(s, m)
                if m:
                    out_y(s - 1, m - 1)

            for s in range(LOOP0):
                step(s, s)
            with dve.Fori(0, LOOPN) as i:
                counter[0] = i
                for u in range(NG):
                    step(NG * i + (LOOP0 + u), LOOP0 + u)
            for s in range(LOOP0 + NG * LOOPN, NS):
                step(s, s)
            out_h(NS - 1, NS - 1)
            out_y(NS - 1, NS - 1)

            def combine(t):
                for k in range(TOPK):
                    n = t * TOPK + k
                    dve.wait_ge(back[n % NG], 16 * (n // NG + 1))
                    ins = nc.vector.scalar_tensor_tensor(out=xs[:, t, :], in0=grow[n % NG][:], scalar=wtop[:, t, k:k + 1],
                                                         in1=xs[:, t, :], op0=ALU.mult, op1=ALU.add)
                    ins.then_inc(back_used, 1)
                    dve.wait_ge(back_used, n + 1)
                nc.vector.engine_nop().then_inc(fin_ready, 1)

            for j in range(SC):
                pair_mul(SC + j)
            for t in range(HALF):
                combine(t)
            add_shared(28, 1)
            dve.wait_ge(ring_out, 32)
            for t in range(HALF, NT):
                combine(t)


_OUT = ((16, 64, 512), 'float32')


def kernel(x, ctx_4096, L0_xattn_Wq, L0_xattn_bq, L0_xattn_Wk, L0_xattn_bk, L0_ffn_gate_w, L0_ffn_w_gate_up,
           L0_ffn_w_down, L0_ffn_shared_w_gate_up, L0_ffn_shared_w_down):
    import numpy as np
    import concourse.bacc as bacc
    from concourse.bass_utils import run_bass_kernel_spmd

    def feature_chunks(a):
        a = np.asarray(a)
        a = a.reshape(a.shape[:-1] + (a.shape[-1] // 128, 128))
        return np.ascontiguousarray(np.moveaxis(a, (-1, -2), (0, 1)))

    def token_tiles(a):
        a = np.asarray(a).reshape(8, 128, 512)
        return np.ascontiguousarray(a.transpose(1, 0, 2))

    gu = np.asarray(L0_ffn_w_gate_up)
    arrays = {
        "x": token_tiles(x),
        "ctx_t": feature_chunks(np.asarray(ctx_4096).reshape(1024, 512)),
        "ctx_n": token_tiles(ctx_4096),
        "wq_t": feature_chunks(L0_xattn_Wq),
        "wk_t": feature_chunks(L0_xattn_Wk),
        "bq": feature_chunks(L0_xattn_bq),
        "bk": feature_chunks(L0_xattn_bk),
        "gate_t": feature_chunks(L0_ffn_gate_w),
        "moe_gu_t": np.ascontiguousarray(feature_chunks(gu).transpose(0, 2, 1, 3)),
        "moe_dn_t": np.ascontiguousarray(np.asarray(L0_ffn_w_down).transpose(2, 0, 1)),
        "sh_gu_t": feature_chunks(L0_ffn_shared_w_gate_up),
        "sh_dn_t": feature_chunks(L0_ffn_shared_w_down),
    }
    nc = bacc.Bacc("TRN2", target_bir_lowering=False, num_devices=1)
    args = [nc.dram_tensor(n, a.shape, mybir.dt.from_np(a.dtype), kind="ExternalInput").ap()
            for n, a in arrays.items()]
    out = nc.dram_tensor("out", (128, 8, 512), F32, kind="ExternalOutput").ap()
    xattn_moe(nc, *args, out)
    r = run_bass_kernel_spmd(nc, [arrays], core_ids=[0])
    got = r.results[0]["out"]
    return np.ascontiguousarray(got.transpose(1, 0, 2)).reshape(_OUT[0])
```

```python
from contextlib import ExitStack

import concourse.bass as bass
from concourse import mybir

F32 = mybir.dt.float32
F32R = mybir.dt.float32r
BF16 = mybir.dt.bfloat16
I32 = mybir.dt.int32
U32 = mybir.dt.uint32
ALU = mybir.AluOpType
ACT = mybir.ActivationFunctionType
AX = mybir.AxisListType

P = 128


def xattn_moe(nc, x, ctx_t, ctx_n, wq_t, wk_t, bq, bk, gate_t, moe_gu_t, moe_dn_t, sh_gu_t, sh_dn_t, out):
    _, NT, D = x.shape
    T = NT * P
    C = D // P
    SEQ = 64
    NE = gate_t.shape[2]
    TOPK = 2
    FE = moe_dn_t.shape[0]
    SC = sh_dn_t.shape[1]
    HALF = NT // 2
    HW = HALF * P
    NS = T * TOPK // P + NE - 1
    SCALE = float(D) ** -0.5
    EPS = 1e-5

    xn_dram = nc.dram_tensor("xn_dram", (T, D), F32, kind="Internal").ap()
    y_dram = nc.dram_tensor("y_dram", (NS * P, D), F32, kind="Internal").ap()

    with ExitStack() as ctx:
        def sb(name, shape, dt=F32):
            return ctx.enter_context(nc.sbuf_tensor(name, shape, dt))

        def sem(name):
            return ctx.enter_context(nc.semaphore(name))

        bank = [ctx.enter_context(nc.psum_tensor(f"bank{i}", [P, 512], F32)) for i in range(8)]

        KB = 1024
        base = (nc.sbuf_base + 63) // 64 * 64
        ctx.enter_context(nc.sbuf_tensor("fence", [P, (base - nc.sbuf_base + 184 * KB) // 4 + 8], F32))

        def at(name, kb, shape, dt=F32):
            return nc.alloc_sbuf_tensor_at(name, shape, dt, offset=base + int(kb * KB))

        GUW = C * 2 * FE
        moe_gu = at("moe_gu", 0, [P, NE * GUW])
        moe_dn = at("moe_dn", 64, [P, NE * D])
        ctxN = at("ctxN", 0, [P, NT, D])
        kT = at("kT", 16, [P, C, T])
        ctx1T = at("ctx1T", 32, [P, 2, C, HW], F32R)
        qT = at("qT", 32, [P, C, T])
        wqT = at("wqT", 48, [P, 2, C, D], F32R)
        wk_raw = at("wk_raw", 64, [P, C, D])
        wq_raw = at("wq_raw", 72, [P, C, D])
        sh_raw = at("sh_raw", 64, [P, C, 2 * SC * P])
        wkT = at("wkT", 96, [P, 2, C, D], F32R)
        ctx_raw = [at(f"ctx_raw{h}", 112 + 8 * h, [P, C, HW]) for h in range(2)]
        sh_gu = [at(f"sh_gu{i}", 96 + 16 * i, [P, C, 2 * SC * P], F32R) for i in range(2)]
        sh_dn = at("sh_dn", 128, [P, SC, D])
        xs = at("xs", 136, [P, NT, D])
        xn = at("xn", 152, [P, NT, D])
        xT = [at("xT0", 80, [P, 2, C, HW], F32R), at("xT1", 168, [P, 2, C, HW], F32R)]
        NG = 4
        grow = [at(f"grow{i}", 152 + 2 * i, [P, D]) for i in range(NG)]
        slothot = at("slothot", 156, [P, NT * TOPK, 2, 32], BF16)
        past = at("past", 158, [1, 32, NE])
        wsp = [at(f"wsp{i}", 96 + 8 * i, [P, 2, C, 2 * FE], F32R) for i in range(2)]
        gT = [at(f"gT{i}", 112 + 4 * i, [P, 2, C, P], F32R) for i in range(2)]
        sg = [at(f"sg{i}", 168 + i / 2, [P, FE]) for i in range(2)]
        hh = [at(f"hh{i}", 169 + i / 2, [P, FE]) for i in range(2)]
        hT = [at(f"hT{i}", 170 + i / 2, [P, P]) for i in range(2)]
        ys = [at(f"ys{i}", 172 + 2 * i, [P, D]) for i in range(2)]
        hsT = [sb("hsT0", [P, SC, HW]), at("hsT1", 160, [P, SC, HW])]
        gate = sb("gate", [P, C, NE])
        gate2 = [sb(f"gate2{i}", [P, C, NE], F32R) for i in range(2)]
        bqs = sb("bqs", [P, C])
        bks = sb("bks", [P, C])
        ident = sb("ident", [P, P])
        before = sb("before", [P, P], BF16)
        ones = sb("ones", [P, P], BF16)
        iota_f = sb("iota_f", [P, P])
        tile_no = sb("tile_no", [P, NT])
        tile_row = sb("tile_row", [P, 1])
        steps128 = sb("steps128", [P, 8])
        lower_e = sb("lower_e", [P, NE, NE])
        neg_half = sb("neg_half", [P, 2 * NT])
        stats = sb("stats", [P, NT, 6])
        meanvar = sb("meanvar", [P, NT, 2])
        vareps = sb("vareps", [P, NT])
        rstd = sb("rstd", [P, NT])
        E = [hsT[0][:, h, :].rearrange("p (t k) -> p t k", t=HALF) for h in range(2)]
        ET = hsT[0][:, 2, :].rearrange("p (t k) -> p t k", t=HALF)
        smax = sb("smax", [P, NT])
        ssum = sb("ssum", [P, NT])
        rsum = sb("rsum", [P, NT])
        silu_s = [sb(f"silu_s{i}", [P, HW]) for i in range(2)]
        rmax = sb("rmax", [P, NT])
        prob = sb("prob", [P, NT, NE])
        psm = sb("psm", [P, NT])
        prs = sb("prs", [P, NT])
        top = sb("top", [P, NT, 8])
        topi = sb("topi", [P, NT, 8], U32)
        topf = sb("topf", [P, NT, TOPK])
        wsum = sb("wsum", [P, NT])
        wrec = sb("wrec", [P, NT])
        wtop = sb("wtop", [P, NT, TOPK])
        pick = [sb(f"pick{k}", [P, NT, NE]) for k in range(TOPK)]
        picked = sb("picked", [P, NT, NE], BF16)
        over = sb("over", [P, NE, 8])
        ntile = sb("ntile", [P, NE])
        prod_e = sb("prod_e", [P, NE, NE])
        first = sb("first", [P, NE])
        place = sb("place", [P, NT, NE])
        placed = [sb(f"placed{k}", [P, NT, NE]) for k in range(TOPK)]
        rows = sb("rows", [P, NT, TOPK])
        rows_i = sb("rows_i", [P, NT, TOPK], I32)
        rows_u = sb("rows_u", [P, NT, TOPK], U32)
        slot_i = sb("slot_i", [P, NT, TOPK], I32)
        slot_f = sb("slot_f", [P, NT, TOPK])
        inrow = sb("inrow", [P, NT, TOPK])
        last_e = sb("last_e", [1, NE])
        slot_e = sb("slot_e", [1, 32])
        slot_exp = sb("slot_exp", [1, 32], I32)
        rowhot = [sb(f"rowhot{i}", [P, P], BF16) for i in range(4)]
        src_tile = sb("src_tile", [P, 32])
        src_rows = sb("src_rows", [P, 32], U32)

        ld = {n: sem(f"ld_{n}") for n in (
            "small", "wk0", "wk", "ctx00", "ctx01", "ctx1", "x0", "x1", "wq", "ctxN", "shgu", "shdn", "dn0", "dn1", "gu0", "gu1", "gu2", "gu3")}
        split_hi = {n: sem(f"hi_{n}") for n in ("wk", "ctx1", "wq", "shgu", "gate")}
        split_lo = {n: sem(f"lo_{n}") for n in ("wk", "ctx1", "wq", "shgu", "gate")}
        const_step = sem("const_step")
        const_ready = sem("const_ready")
        dve_step = sem("dve_step")
        zeroed = sem("zeroed")
        var_ready = sem("var_ready")
        rstd_ready = sem("rstd_ready")
        xn_ready = sem("xn_ready")
        xn_stored = sem("xn_stored")
        proj_done = sem("proj_done")
        proj_out = sem("proj_out")
        ring_done = sem("ring_done")
        ring_hi = sem("ring_hi")
        ring_out = sem("ring_out")
        score_done = sem("score_done")
        shifted = sem("shifted")
        exp_done = sem("exp_done")
        exp_half = sem("exp_half")
        shift_half = sem("shift_half")
        et_done = sem("et_done")
        et_out = sem("et_out")
        logit_done = sem("logit_done")
        rshift = sem("rshift")
        rexp = sem("rexp")
        gate_done = sem("gate_done")
        up_done = sem("up_done")
        pair_silu = sem("pair_silu")
        pair_out = sem("pair_out")
        picked_ready = sem("picked_ready")
        count_done = sem("count_done")
        exp_table = sem("exp_table")
        slothot_ready = sem("slothot_ready")
        rowhot_ready = sem("rowhot_ready")
        rowhot_used = sem("rowhot_used")
        src_ready = sem("src_ready")
        rows_ready = sem("rows_ready")
        gathered = [sem(f"gathered{i}") for i in range(NG)]
        turned = sem("turned")
        w_hi = sem("w_hi")
        w_lo = sem("w_lo")
        gT_hi = sem("gT_hi")
        gT_out = sem("gT_out")
        gu_done = sem("gu_done")
        silu_done = sem("silu_done")
        h_ready = sem("h_ready")
        h_turned = sem("h_turned")
        hT_out = sem("hT_out")
        y_done = sem("y_done")
        y_out = sem("y_out")
        y_stored = [sem(f"y_stored{i}") for i in range(2)]
        back = [sem(f"back{i}") for i in range(NG)]
        back_used = sem("back_used")
        stored = sem("stored")

        LOOP0 = 4
        LOOPN = (NS - 1 - LOOP0) // NG

        def slot_steps(eng, step):
            for s in range(LOOP0):
                step(s, s)
            with eng.Fori(0, LOOPN) as i:
                for u in range(NG):
                    step(NG * i + (LOOP0 + u), LOOP0 + u)
            for s in range(LOOP0 + NG * LOOPN, NS):
                step(s, s)

        def ge(eng, s, value):
            if not isinstance(value, int) or value > 0:
                eng.wait_ge(s, value)

        def expert_of(eng, s):
            src = slot_exp[0:1, s:s + 1] if isinstance(s, int) else slot_exp[0:1, bass.ds(s, 1)]
            return eng.value_load(src, min_val=0, max_val=NE - 1)

        def raw_gu(e, a):
            return moe_gu[:, bass.ds(e * GUW + a * 2 * FE, 4 * FE)].rearrange("p (c i) -> p c i", c=2)

        block = ctx.enter_context(nc.Block())

        @block.sync
        def _(sp):
            def load(name, dst, src):
                sp.dma_start(dst, src).then_inc(ld[name], 16)

            load("wk0", wk_raw[:, :, 0:P], wk_t[:, :, 0:P])
            load("ctx01", ctx_raw[0][:, 2:4], ctx_t[:, 2:4, 0:HW])
            load("wk", wk_raw[:, :, P:D], wk_t[:, :, P:D])
            load("x0", xs[:, 0:HALF, :], x[:, 0:HALF, :])
            load("small", bqs[:], bq)
            load("small", bks[:], bk)
            load("small", gate[:], gate_t)
            load("ctx1", ctx_raw[1][:], ctx_t[:, :, HW:T])
            load("wq", wq_raw[:], wq_t)
            load("x1", xs[:, HALF:NT, :], x[:, HALF:NT, :])
            load("ctxN", ctxN[:], ctx_n)
            load("shdn", sh_dn[:], sh_dn_t)
            sp.wait_ge(proj_done, 4)
            sp.wait_ge(split_lo["wk"], 1)
            sp.wait_ge(split_lo["wq"], 1)
            load("shgu", sh_raw[:], sh_gu_t)
            gu_flat = moe_gu_t.rearrange("p e c i -> p (e c i)")
            dn_flat = moe_dn_t.rearrange("p e d -> p (e d)")
            sp.wait_ge(proj_done, 16)
            load("gu3", moe_gu[:, 12288:16384], gu_flat[:, 12288:16384])
            sp.wait_ge(split_lo["shgu"], 2)
            load("dn0", moe_dn[:, 0:4096], dn_flat[:, 0:4096])
            sp.wait_ge(score_done, 2)
            load("gu1", moe_gu[:, 4096:8192], gu_flat[:, 4096:8192])
            load("gu2", moe_gu[:, 8192:12288], gu_flat[:, 8192:12288])
            sp.wait_ge(ring_done, 20)
            load("gu0", moe_gu[:, 0:4096], gu_flat[:, 0:4096])
            for h in range(2):
                sp.wait_ge(xn_ready, NT + HALF * (h + 1))
                sp.dma_start(xn_dram[h * HW:(h + 1) * HW, :].rearrange("(t p) d -> p t d", p=P),
                             xn[:, h * HALF:(h + 1) * HALF, :]).then_inc(xn_stored, 16)

            def store(s, m):
                sp.wait_ge(y_out, s + 1)
                dst = y_dram[bass.ds(s * P, P), :] if not isinstance(s, int) else y_dram[s * P:(s + 1) * P, :]
                sp.dma_start(dst, ys[m % 2][:]).then_inc(y_stored[m % 2], 16)

            sp.wait_ge(logit_done, 1)
            sp.wait_ge(up_done, SC)
            load("dn1", moe_dn[:, 4096:8192], dn_flat[:, 4096:8192])
            slot_steps(sp, store)
            for t in range(NT):
                sp.wait_ge(back_used, TOPK * (t + 1))
                sp.wait_ge(ring_out, 24 + t + 1)
                sp.dma_start(out[:, t, :], xs[:, t, :]).then_inc(stored, 16)
            sp.wait_ge(stored, 16 * NT)

        @block.gpsimd
        def _(pool):
            steps = [0]

            def then(ins):
                steps[0] += 1
                ins.then_inc(const_step, 1)
                pool.wait_ge(const_step, steps[0])

            nc.gpsimd.memset(neg_half[:], -0.5).then_inc(const_ready, 1)
            then(nc.gpsimd.memset(ident[:], 0.0))
            nc.gpsimd.affine_select(out=ident[:], in_=ident[:], compare_op=ALU.not_equal, fill=1.0, base=0,
                                    pattern=[[-1, P]], channel_multiplier=1).then_inc(const_ready, 1)
            for h in range(2):
                then(nc.gpsimd.memset(E[h], 0.0))
            nc.gpsimd.memset(ones[:], 1.0).then_inc(const_ready, 1)

            def rsqrt(n, a, b):
                pool.wait_ge(var_ready, n)
                nc.gpsimd.tensor_tensor(out=rstd[:, a:b], in0=vareps[:, a:b], in1=neg_half[:, a:b],
                                        op=ALU.pow).then_inc(rstd_ready, 1)

            pool.wait_ge(const_ready, 3)

            def lo_of(name, n, lo, raw, hi):
                pool.wait_ge(split_hi[name], n)
                nc.gpsimd.tensor_tensor(out=lo, in0=raw, in1=hi.bitcast(F32), op=ALU.subtract).then_inc(split_lo[name], 1)

            rsqrt(1, 0, HALF)
            lo_of("wq", 1, wqT[:, 1], wq_raw[:], wqT[:, 0])
            lo_of("gate", 1, gate2[1][:], gate[:], gate2[0][:])
            rsqrt(2, HALF, NT)
            then(nc.gpsimd.memset(before[:], 1.0))
            nc.gpsimd.affine_select(out=before[:], in_=before[:], compare_op=ALU.is_gt, fill=0.0, base=0,
                                    pattern=[[1, P]], channel_multiplier=-1).then_inc(const_ready, 1)
            nc.gpsimd.iota(iota_f[:], pattern=[[1, P]], base=0, channel_multiplier=0,
                           allow_small_or_imprecise_dtypes=True).then_inc(const_ready, 1)
            nc.gpsimd.iota(tile_no[:], pattern=[[1, NT]], base=0, channel_multiplier=0,
                           allow_small_or_imprecise_dtypes=True).then_inc(const_ready, 1)
            nc.gpsimd.iota(tile_row[:], pattern=[[0, 1]], base=0, channel_multiplier=1,
                           allow_small_or_imprecise_dtypes=True).then_inc(const_ready, 1)
            nc.gpsimd.iota(steps128[:], pattern=[[P, 8]], base=0, channel_multiplier=0,
                           allow_small_or_imprecise_dtypes=True).then_inc(const_ready, 1)
            then(nc.gpsimd.memset(lower_e[:], 1.0))
            nc.gpsimd.affine_select(out=lower_e[:], in_=lower_e[:], compare_op=ALU.is_gt, fill=0.0, base=0,
                                    pattern=[[1, NE], [-1, NE]], channel_multiplier=0).then_inc(const_ready, 1)
            for i in range(2):
                lo_of("shgu", i + 1, sh_gu[1][:, 2 * i:2 * i + 2], sh_raw[:, 2 * i:2 * i + 2], sh_gu[0][:, 2 * i:2 * i + 2])
            rsqrt(3, 0, HALF)
            rsqrt(4, HALF, NT)
            pool.wait_ge(src_ready, 1)
            pool.wait_ge(xn_stored, 32)
            for s in range(NS):
                ge(pool, turned, s - NG + 1)
                nc.gpsimd.indirect_dma_start(
                    out=grow[s % NG][:], out_offset=None, in_=xn_dram,
                    in_offset=bass.IndirectOffsetOnAxis(ap=src_rows[:, s:s + 1], axis=0),
                ).then_inc(gathered[s % NG], 16)
            pool.wait_ge(turned, NS)
            pool.wait_ge(y_stored[0], 16 * ((NS + 1) // 2))
            pool.wait_ge(y_stored[1], 16 * (NS // 2))
            pool.wait_ge(rows_ready, 1)
            for n in range(NT * TOPK):
                t, k = n // TOPK, n % TOPK
                ge(pool, back_used, n - NG + 1)
                nc.gpsimd.indirect_dma_start(
                    out=grow[n % NG][:], out_offset=None, in_=y_dram,
                    in_offset=bass.IndirectOffsetOnAxis(ap=rows_u[:, t, k:k + 1], axis=0),
                ).then_inc(back[n % NG], 16)

        @block.tensor
        def _(pe):
            def mm(o, w, m, start, stop):
                return nc.tensor.matmul(o, w, m, start=start, stop=stop)

            def mm3(o, w, m, start, stop):
                mm(o, w(0), m(0), start, False)
                mm(o, w(0), m(1), False, False)
                return mm(o, w(1), m(0), False, stop)

            def project_raw(o):
                for c in range(C):
                    if o == 0 and c == 2:
                        pe.wait_ge(ld["ctx01"], 16)
                    last = mm(bank[o][:], wk_raw[:, c, o * P:(o + 1) * P], ctx_raw[0][:, c, :], c == 0, c == C - 1)
                last.then_inc(proj_done, 1)

            def project(n, w, mov, o):
                pe.wait_ge(proj_out, n - 3)
                for c in range(C):
                    last = mm3(bank[n % 4][:], lambda i: w[:, i, c, o * P:(o + 1) * P], lambda i: mov[:, i, c, :],
                               c == 0, c == C - 1)
                last.then_inc(proj_done, 1)

            def ring(m):
                if m >= 2:
                    pe.wait_ge(ring_out, m - 1)
                return bank[4 + m % 2]

            def turn_xn(m, h, xn_before, js):
                for j in js:
                    t = h * HALF + j
                    pe.wait_ge(xn_ready, xn_before + t + 1)
                    b = ring(m + j)
                    for c in range(C):
                        last = nc.tensor.transpose(b[:, c * P:(c + 1) * P], xn[:, t, c * P:(c + 1) * P], ident[:])
                    last.then_inc(ring_done, 1)

            def scores(h):
                pe.wait_ge(proj_out, 12 + 4 * h)
                if h:
                    pe.wait_ge(shifted, 1)
                for j in range(HALF):
                    a = (h * HALF + j) * P
                    for c in range(C):
                        last = mm(bank[6][:, j * P:(j + 1) * P], qT[:, c, a:a + P], kT[:, c, a:a + P],
                                  c == 0, c == C - 1)
                last.then_inc(score_done, 1)

            def turn_exp(h):
                pe.wait_ge(exp_done, h + 1)
                if h:
                    pe.wait_ge(et_out, 1)
                for j in range(HALF):
                    last = nc.tensor.transpose(bank[7][:, j * P:(j + 1) * P], E[h][:, j, :], ident[:])
                last.then_inc(et_done, 1)

            def attend(m, h, js):
                pe.wait_ge(et_out, h + 1)
                pe.wait_ge(ld["ctxN"], 16)
                for j in js:
                    b = ring(m + j)
                    mm(b[:], ET[:, j, :], ctxN[:, h * HALF + j, :], True, True).then_inc(ring_done, 1)

            def shared(h, j, g):
                n = h * SC + j
                if n >= 2:
                    pe.wait_ge(pair_out, n - 1)
                a = g * SC * P + j * P
                for c in range(C):
                    last = mm3(bank[2 * (n % 2) + g][:], lambda i: sh_gu[i][:, c, a:a + P],
                               lambda i: xT[h][:, i, c, :], c == 0, c == C - 1)
                last.then_inc((gate_done, up_done)[g], 1)

            def shared_down(m, h, js):
                pe.wait_ge(pair_out, (h + 1) * SC)
                pe.wait_ge(ld["shdn"], 16)
                for j in js:
                    b = ring(m + j)
                    for c in range(SC):
                        last = mm(b[:], hsT[h][:, c, j * P:(j + 1) * P], sh_dn[:, c, :], c == 0, c == SC - 1)
                    last.then_inc(ring_done, 1)

            pe.wait_ge(ld["wk0"], 16)
            pe.wait_ge(ld["ctx00"], 16)
            project_raw(0)
            pe.wait_ge(ld["wk"], 16)
            for o in range(1, C):
                project_raw(o)
            pe.wait_ge(const_ready, 2)
            turn_xn(0, 0, 0, (0, 1))
            pe.wait_ge(split_lo["wk"], 1)
            pe.wait_ge(split_lo["ctx1"], 1)
            project(4, wkT, ctx1T, 0)
            turn_xn(0, 0, 0, (2, 3))
            for o in range(1, C):
                project(4 + o, wkT, ctx1T, o)
            pe.wait_ge(split_lo["wq"], 1)
            pe.wait_ge(ring_out, 4)
            project(8, wqT, xT[0], 0)
            turn_xn(4, 1, 0, (0, 1))
            project(9, wqT, xT[0], 1)
            turn_xn(4, 1, 0, (2, 3))
            project(10, wqT, xT[0], 2)
            project(11, wqT, xT[0], 3)
            pe.wait_ge(ring_out, 8)
            project(12, wqT, xT[1], 0)
            scores(0)
            project(13, wqT, xT[1], 1)
            turn_exp(0)
            project(14, wqT, xT[1], 2)
            attend(8, 0, (0, 1))
            project(15, wqT, xT[1], 3)
            attend(8, 0, (2, 3))
            scores(1)
            turn_xn(12, 0, NT, (0, 1, 2, 3))
            pe.wait_ge(ring_out, 16)
            pe.wait_ge(proj_out, 16)
            pe.wait_ge(split_lo["shgu"], 2)
            shared(0, 0, 0)
            turn_exp(1)
            shared(0, 0, 1)
            attend(16, 1, (0, 1, 2, 3))
            shared(0, 1, 0)
            shared(0, 1, 1)
            turn_xn(20, 1, NT, (0, 1))
            shared(0, 2, 0)
            turn_xn(20, 1, NT, (2, 3))
            shared(0, 2, 1)
            pe.wait_ge(ring_out, 24)
            pe.wait_ge(split_lo["gate"], 1)
            pe.wait_ge(shifted, 2)
            for t in range(NT):
                a = t % HALF * P
                for c in range(C):
                    last = mm3(bank[6][:, t * NE:(t + 1) * NE], lambda i: xT[t // HALF][:, i, c, a:a + P],
                               lambda i: gate2[i][:, c, :], c == 0, c == C - 1)
            last.then_inc(logit_done, 1)
            shared(0, 3, 0)
            shared(0, 3, 1)
            pe.wait_ge(picked_ready, 1)
            pe.wait_ge(const_ready, 9)
            W = NT * NE
            pk = picked[:].rearrange("p t e -> p (t e)")
            mm(bank[7][:, 0:W], before[:], pk, True, False)
            for d in range(1, NT):
                mm(bank[7][:, d * NE:W], ones[:], pk[:, 0:W - d * NE], False, d == NT - 1)
            for t in range(NT):
                last = mm(bank[6][:, 256:256 + NE], ones[:], picked[:, t, :], t == 0, t == NT - 1)
            last.then_inc(count_done, 1)
            for j in range(2):
                for g in range(2):
                    shared(1, j, g)
            pe.wait_ge(slothot_ready, 2)
            for n in range(NT * TOPK):
                pe.wait_ge(rowhot_ready, n + 1)
                mm(bank[7][:, 256:320], rowhot[n % 4][:], slothot[:, n].rearrange("p a s -> p (a s)"), n == 0,
                   n == NT * TOPK - 1).then_inc(rowhot_used, 1)
            for j in range(2, SC):
                for g in range(2):
                    shared(1, j, g)
            shared_down(24, 0, (0, 1))

            pe.wait_ge(exp_table, 1)
            for n in ("dn0", "dn1", "gu0", "gu1", "gu2", "gu3"):
                pe.wait_ge(ld[n], 16)

            def turn(s, m):
                g = m % NG
                pe.wait_ge(gathered[g], 16 * ((s - g) // NG + 1) if isinstance(s, int) else loop_turn(s, m))
                ge(pe, gT_out, s - 1)
                b = bank[4 + m % 2]
                for c in range(C):
                    last = nc.tensor.transpose(b[:, c * P:(c + 1) * P], grow[g][:, c * P:(c + 1) * P], ident[:])
                last.then_inc(turned, 1)

            def gate_up(s, m, chunks):
                if 0 in chunks:
                    pe.wait_ge(gT_out, s + 1)
                    ge(pe, h_ready, s - 1)
                pe.wait_ge(w_lo, 2 * s + (1 if 0 in chunks else 2))
                for c in chunks:
                    last = mm3(bank[m % 2][:, 0:2 * FE], lambda i: gT[m % 2][:, i, c, :],
                               lambda i: wsp[m % 2][:, i, c, :], c == 0, c == C - 1)
                if C - 1 in chunks:
                    last.then_inc(gu_done, 1)

            def turn_h(s, m):
                pe.wait_ge(h_ready, s + 1)
                ge(pe, hT_out, s - 1)
                nc.tensor.transpose(bank[2 + m % 2][:, 0:P], hh[m % 2][:], ident[:]).then_inc(h_turned, 1)

            def down(s, m, e):
                pe.wait_ge(hT_out, s + 1)
                ge(pe, y_out, s - 1)
                mm(bank[6 + m % 2][:], hT[m % 2][:], moe_dn[:, bass.ds(e * D, D)], True, True).then_inc(y_done, 1)

            counter = [None]

            def loop_turn(s, m):
                return 16 * counter[0] + 16 * (m // NG + 1)

            def step(s, m):
                more = not (isinstance(s, int) and s + 1 >= NS)
                if m:
                    e = expert_of(pe, s - 1)
                if more:
                    turn(s + 1, m + 1)
                gate_up(s, m, (0, 1))
                if m:
                    turn_h(s - 1, m - 1)
                gate_up(s, m, (2, 3))
                if m:
                    down(s - 1, m - 1, e)

            pe.wait_ge(ring_out, 26)
            pe.wait_ge(pair_out, 2 * SC)
            pe.wait_ge(src_ready, 1)
            turn(0, 0)
            for s in range(LOOP0):
                step(s, s)
            with pe.Fori(0, LOOPN) as i:
                counter[0] = i
                for u in range(NG):
                    step(NG * i + (LOOP0 + u), LOOP0 + u)
            for s in range(LOOP0 + NG * LOOPN, NS):
                step(s, s)
            turn_h(NS - 1, NS - 1)
            down(NS - 1, NS - 1, expert_of(pe, NS - 1))

            shared_down(24, 0, (2, 3))
            shared_down(28, 1, range(HALF))

        @block.scalar
        def _(act):
            act.dma_start(ctx_raw[0][:, 0:2], ctx_t[:, 0:2, 0:HW]).then_inc(ld["ctx00"], 16)

            def proj_evac(n, dst, bias, h, o):
                if n == 0:
                    act.wait_ge(ld["small"], 48)
                act.wait_ge(proj_done, n + 1)
                nc.scalar.activation(dst[:, o, h * HW:(h + 1) * HW], bank[n % 4][:], ACT.Identity,
                                     bias=bias[:, o:o + 1]).then_inc(proj_out, 1)

            def hi_of(name, hi, raw):
                act.wait_ge(ld[name], 16)
                nc.scalar.copy(hi, raw).then_inc(split_hi[name], 1)

            def xT_hi(m, h, js):
                for j in js:
                    act.wait_ge(ring_done, m + j + 1)
                    nc.scalar.copy(xT[h][:, 0, :, j * P:(j + 1) * P],
                                   bank[4 + (m + j) % 2][:].rearrange("p (c t) -> p c t", c=C)).then_inc(ring_hi, 1)

            def softmax_exp(h):
                act.wait_ge(shifted, h + 1)
                for b in range(2):
                    r = slice(b * SEQ, (b + 1) * SEQ)
                    last = nc.scalar.activation(E[h][r, :, r], E[h][r, :, r], ACT.Exp, scale=SCALE)
                    if b == 0:
                        last.then_inc(exp_half, 1)
                last.then_inc(exp_done, 1)

            def et_evac(h):
                act.wait_ge(et_done, h + 1)
                if h:
                    act.wait_ge(ring_done, 12)
                nc.scalar.copy(ET, bank[7][:].rearrange("p (t k) -> p t k", t=HALF)).then_inc(et_out, 1)

            def pair_silu_step(n):
                act.wait_ge(gate_done, n + 1)
                if n >= 2:
                    act.wait_ge(pair_out, n - 1)
                nc.scalar.activation(silu_s[n % 2][:], bank[2 * (n % 2)][:], ACT.Silu).then_inc(pair_silu, 1)

            act.wait_ge(ld["wk0"], 16)
            hi_of("wk", wkT[:, 0], wk_raw[:])
            proj_evac(0, kT, bks, 0, 0)
            nc.scalar.copy(gate2[0][:], gate[:]).then_inc(split_hi["gate"], 1)
            proj_evac(1, kT, bks, 0, 1)
            hi_of("ctx1", ctx1T[:, 0], ctx_raw[1][:])
            proj_evac(2, kT, bks, 0, 2)
            hi_of("wq", wqT[:, 0], wq_raw[:])
            proj_evac(3, kT, bks, 0, 3)
            xT_hi(0, 0, (0, 1))
            proj_evac(4, kT, bks, 1, 0)
            xT_hi(0, 0, (2, 3))
            for o in range(1, C):
                proj_evac(4 + o, kT, bks, 1, o)
            proj_evac(8, qT, bqs, 0, 0)
            xT_hi(4, 1, (0, 1))
            proj_evac(9, qT, bqs, 0, 1)
            xT_hi(4, 1, (2, 3))
            proj_evac(10, qT, bqs, 0, 2)
            act.wait_ge(proj_done, 8)
            hi_of("shgu", sh_gu[0][:, 0:2], sh_raw[:, 0:2])
            proj_evac(11, qT, bqs, 0, 3)
            hi_of("shgu", sh_gu[0][:, 2:4], sh_raw[:, 2:4])
            proj_evac(12, qT, bqs, 1, 0)
            softmax_exp(0)
            proj_evac(13, qT, bqs, 1, 1)
            et_evac(0)
            proj_evac(14, qT, bqs, 1, 2)
            proj_evac(15, qT, bqs, 1, 3)
            softmax_exp(1)
            xT_hi(12, 0, (0, 1, 2, 3))
            et_evac(1)
            pair_silu_step(0)
            pair_silu_step(1)
            xT_hi(20, 1, (0, 1))
            pair_silu_step(2)
            xT_hi(20, 1, (2, 3))
            act.wait_ge(rshift, 1)
            nc.scalar.activation(prob[:], prob[:], ACT.Exp).then_inc(rexp, 1)
            for n in range(3, 2 * SC):
                pair_silu_step(n)

            act.wait_ge(exp_table, 1)
            for n in ("gu0", "gu1", "gu2", "gu3"):
                act.wait_ge(ld[n], 16)
            act.wait_ge(up_done, 2 * SC)

            def weights_hi(s, m, e):
                ge(act, gu_done, s - 1)
                nc.scalar.copy(wsp[m % 2][:, 0], moe_gu[:, bass.ds(e * GUW, GUW)].rearrange("p (c i) -> p c i", c=C))\
                    .then_inc(w_hi, 1)

            def tokens_hi(s, m):
                act.wait_ge(turned, s + 1)
                ge(act, gu_done, s - 1)
                nc.scalar.copy(gT[m % 2][:, 0], bank[4 + m % 2][:].rearrange("p (c t) -> p c t", c=C))\
                    .then_inc(gT_hi, 1)

            counter = [None]

            def out_y(s, m):
                act.wait_ge(y_done, s + 1)
                if isinstance(s, int):
                    ge(act, y_stored[m % 2], 16 * (s // 2))
                else:
                    act.wait_ge(y_stored[m % 2], 32 * counter[0] + 16 * (m // 2))
                nc.scalar.copy(ys[m % 2][:], bank[6 + m % 2][:]).then_inc(y_out, 1)

            def step(s, m):
                if m >= 2:
                    out_y(s - 2, m - 2)
                if not (isinstance(s, int) and s + 1 >= NS):
                    tokens_hi(s + 1, m + 1)
                if not (isinstance(s, int) and s + 2 >= NS):
                    e = expert_of(act, s + 2)
                act.wait_ge(gu_done, s + 1)
                ge(act, h_ready, s - 1)
                nc.scalar.activation(sg[m % 2][:], bank[m % 2][:, 0:FE], ACT.Silu).then_inc(silu_done, 1)
                if not (isinstance(s, int) and s + 2 >= NS):
                    weights_hi(s + 2, m + 2, e)

            weights_hi(0, 0, expert_of(act, 0))
            tokens_hi(0, 0)
            weights_hi(1, 1, expert_of(act, 1))
            for s in range(LOOP0):
                step(s, s)
            with act.Fori(0, LOOPN) as i:
                counter[0] = i
                for u in range(NG):
                    step(NG * i + (LOOP0 + u), LOOP0 + u)
            for s in range(LOOP0 + NG * LOOPN, NS):
                step(s, s)
            out_y(NS - 2, NS - 2)
            out_y(NS - 1, NS - 1)

        @block.vector
        def _(dve):
            steps = [0]

            def then(ins):
                steps[0] += 1
                ins.then_inc(dve_step, 1)
                dve.wait_ge(dve_step, steps[0])

            def bn(t):
                then(nc.vector.bn_stats(stats[:, t, :], xs[:, t, :]))
                then(nc.vector.bn_aggr(meanvar[:, t, :], stats[:, t, :]))

            def var(h):
                a, b = h * HALF, (h + 1) * HALF
                nc.vector.tensor_scalar(vareps[:, a:b], meanvar[:, a:b, 1], EPS, None, ALU.add).then_inc(var_ready, 1)

            def lo_of(name, lo, raw, hi):
                dve.wait_ge(split_hi[name], 1)
                nc.vector.tensor_tensor(lo, raw, hi.bitcast(F32), ALU.subtract).then_inc(split_lo[name], 1)

            def normalise(n, h):
                dve.wait_ge(rstd_ready, n)
                for t in range(h * HALF, (h + 1) * HALF):
                    nc.vector.tensor_scalar(xn[:, t, :], xs[:, t, :], meanvar[:, t, 0:1], rstd[:, t:t + 1],
                                            ALU.subtract, ALU.mult).then_inc(xn_ready, 1)

            def xT_lo(m, h, js):
                for j in js:
                    dve.wait_ge(ring_hi, hi_count(m, j))
                    nc.vector.tensor_tensor(xT[h][:, 1, :, j * P:(j + 1) * P],
                                            bank[4 + (m + j) % 2][:].rearrange("p (c t) -> p c t", c=C),
                                            xT[h][:, 0, :, j * P:(j + 1) * P].bitcast(F32), ALU.subtract)\
                        .then_inc(ring_out, 1)

            def hi_count(m, j):
                return {0: 0, 4: 4, 12: 8, 20: 12}[m] + j + 1

            def softmax_shift(h):
                dve.wait_ge(score_done, h + 1)
                s = bank[6][:].rearrange("p (t k) -> p t k", t=HALF)
                mx = smax[:, h * HALF:(h + 1) * HALF]
                for b in range(2):
                    r = slice(b * SEQ, (b + 1) * SEQ)
                    then(nc.vector.tensor_reduce(mx[r, :], s[r, :, r], AX.X, ALU.max))
                for b in range(2):
                    r = slice(b * SEQ, (b + 1) * SEQ)
                    last = nc.vector.tensor_tensor(E[h][r, :, r], s[r, :, r],
                                                   mx[r, :].unsqueeze(2).to_broadcast([SEQ, HALF, SEQ]), ALU.subtract)
                    if b == 0:
                        last.then_inc(shift_half, 1)
                last.then_inc(shifted, 1)

            def softmax_sum(h):
                dve.wait_ge(exp_done, h + 1)
                dve.wait_ge(exp_half, h + 1)
                a, b = h * HALF, (h + 1) * HALF
                then(nc.vector.tensor_reduce(ssum[:, a:b], E[h], AX.X, ALU.add))
                then(nc.vector.reciprocal(rsum[:, a:b], ssum[:, a:b]))

            def residual(m, h, js):
                for j in js:
                    t = h * HALF + j
                    dve.wait_ge(ring_done, m + j + 1)
                    nc.vector.scalar_tensor_tensor(out=xs[:, t, :], in0=bank[4 + (m + j) % 2][:],
                                                   scalar=rsum[:, t:t + 1], in1=xs[:, t, :],
                                                   op0=ALU.mult, op1=ALU.add).then_inc(ring_out, 1)
                for j in js:
                    dve.wait_ge(ring_out, m + j + 1)
                    bn(h * HALF + j)

            def pair_mul(n):
                dve.wait_ge(pair_silu, n + 1)
                dve.wait_ge(up_done, n + 1)
                nc.vector.tensor_tensor(hsT[n // SC][:, n % SC, :], bank[2 * (n % 2) + 1][:], silu_s[n % 2][:], ALU.mult)\
                    .then_inc(pair_out, 1)

            def add_shared(m, j, t):
                dve.wait_ge(ring_done, m + j + 1)
                return nc.vector.tensor_tensor(xs[:, t, :], bank[4 + (m + j) % 2][:], xs[:, t, :], ALU.add)

            for h in range(2):
                dve.wait_ge(ld[f"x{h}"], 16)
                for t in range(h * HALF, (h + 1) * HALF):
                    bn(t)
                var(h)
                if h == 0:
                    lo_of("wk", wkT[:, 1], wk_raw[:], wkT[:, 0])
                    normalise(1, 0)
                    lo_of("ctx1", ctx1T[:, 1], ctx_raw[1][:], ctx1T[:, 0])
                    xT_lo(0, 0, range(HALF))
            normalise(2, 1)
            xT_lo(4, 1, range(HALF))
            dve.wait_ge(const_step, 3)
            softmax_shift(0)
            softmax_sum(0)
            residual(8, 0, (0, 1))
            residual(8, 0, (2, 3))
            var(0)
            softmax_shift(1)
            normalise(3, 0)
            softmax_sum(1)
            xT_lo(12, 0, range(HALF))
            pair_mul(0)
            residual(16, 1, range(HALF))
            var(1)
            pair_mul(1)
            normalise(4, 1)
            xT_lo(20, 1, range(HALF))
            pair_mul(2)

            dve.wait_ge(logit_done, 1)
            dve.wait_ge(const_ready, 9)
            lg = bank[6][:, 0:NT * NE].rearrange("p (t e) -> p t e", t=NT)

            def over_e(ap):
                return ap.unsqueeze(2).to_broadcast([P, NT, NE])

            then(nc.vector.tensor_reduce(rmax[:], lg, AX.X, ALU.max))
            nc.vector.tensor_tensor(prob[:], lg, over_e(rmax[:]), ALU.subtract).then_inc(rshift, 1)
            dve.wait_ge(rexp, 1)
            then(nc.vector.tensor_reduce(psm[:], prob[:], AX.X, ALU.add))
            then(nc.vector.reciprocal(prs[:], psm[:]))
            then(nc.vector.tensor_tensor(prob[:], prob[:], over_e(prs[:]), ALU.mult))
            for t in range(NT):
                then(nc.vector.max(top[:, t, :], prob[:, t, :]))
            for t in range(NT):
                then(nc.vector.max_index(topi[:, t, :], top[:, t, :], prob[:, t, :]))
            then(nc.vector.tensor_copy(topf[:], topi[:, :, 0:TOPK]))
            it = iota_f[:, 0:NE].unsqueeze(1).to_broadcast([P, NT, NE])
            for k in range(TOPK):
                then(nc.vector.tensor_tensor(pick[k][:], it, over_e(topf[:, :, k]), ALU.is_equal))
            nc.vector.tensor_tensor(picked[:], pick[0][:], pick[1][:], ALU.add).then_inc(picked_ready, 1)
            then(nc.vector.tensor_tensor(wsum[:], top[:, :, 0], top[:, :, 1], ALU.add))
            then(nc.vector.reciprocal(wrec[:], wsum[:]))
            then(nc.vector.tensor_tensor(wtop[:], top[:, :, 0:TOPK], wrec[:].unsqueeze(2).to_broadcast([P, NT, TOPK]),
                                         ALU.mult))
            pair_mul(3)
            dve.wait_ge(count_done, 1)
            then(nc.vector.tensor_tensor(over[:], bank[6][:, 256:256 + NE].unsqueeze(2).to_broadcast([P, NE, 8]),
                                         steps128[:].unsqueeze(1).to_broadcast([P, NE, 8]), ALU.is_gt))
            then(nc.vector.tensor_reduce(ntile[:], over[:], AX.X, ALU.add))
            then(nc.vector.tensor_tensor(prod_e[:], lower_e[:], ntile[:].unsqueeze(1).to_broadcast([P, NE, NE]),
                                         ALU.mult))
            then(nc.vector.tensor_reduce(first[:], prod_e[:], AX.X, ALU.add))
            then(nc.vector.scalar_tensor_tensor(out=place[:], in0=first[:].unsqueeze(1).to_broadcast([P, NT, NE]),
                                                scalar=float(P),
                                                in1=bank[7][:, 0:NT * NE].rearrange("p (t e) -> p t e", t=NT),
                                                op0=ALU.mult, op1=ALU.add))
            for k in range(TOPK):
                then(nc.vector.tensor_tensor(placed[k][:], pick[k][:], place[:], ALU.mult))
            for k in range(TOPK):
                then(nc.vector.tensor_reduce(rows[:, :, k], placed[k][:], AX.X, ALU.add))
            then(nc.vector.tensor_copy(rows_i[:], rows[:]))
            nc.vector.tensor_copy(rows_u[:], rows[:]).then_inc(rows_ready, 1)
            then(nc.vector.tensor_scalar(slot_i[:], rows_i[:], 7, None, ALU.arith_shift_right))
            then(nc.vector.tensor_copy(slot_f[:], slot_i[:]))
            then(nc.vector.scalar_tensor_tensor(out=inrow[:], in0=slot_f[:], scalar=-float(P), in1=rows[:],
                                                op0=ALU.mult, op1=ALU.add))
            R = NT * TOPK
            sf = slot_f[:].rearrange("p t k -> p (t k)")
            ir = inrow[:].rearrange("p t k -> p (t k)")
            dve.wait_ge(xn_stored, 32)
            pair_mul(4)
            its = iota_f[:, 0:32].unsqueeze(1).to_broadcast([P, R, 32])
            sfs = sf.unsqueeze(2).to_broadcast([P, R, 32])
            then(nc.vector.tensor_tensor(slothot[:, :, 0, :], its, sfs, ALU.is_equal))
            nc.vector.tensor_tensor(slothot[:, :, 1, :].rearrange("p (t k) s -> p t k s", k=TOPK),
                                    slothot[:, :, 0, :].rearrange("p (t k) s -> p t k s", k=TOPK),
                                    tile_no[:].unsqueeze(2).unsqueeze(3).to_broadcast([P, NT, TOPK, 32]), ALU.mult)\
                .then_inc(slothot_ready, 1)
            dve.wait_ge(slothot_ready, 1)
            nc.vector.tensor_scalar(slothot[:, :, 0, :], slothot[:, :, 0, :], tile_row[:, 0:1], None, ALU.mult)\
                .then_inc(slothot_ready, 1)
            for n in range(R):
                if n >= 4:
                    dve.wait_ge(rowhot_used, n - 3)
                nc.vector.tensor_scalar(rowhot[n % 4][:], iota_f[:], ir[:, n:n + 1], None, ALU.is_equal)\
                    .then_inc(rowhot_ready, 1)
            pair_mul(5)
            then(nc.vector.tensor_tensor(last_e[:], first[0:1, :], ntile[0:1, :], ALU.add))
            then(nc.vector.tensor_tensor(past[:], last_e[:].unsqueeze(1).to_broadcast([1, 32, NE]),
                                         iota_f[0:1, 0:32].unsqueeze(2).to_broadcast([1, 32, NE]), ALU.is_le))
            then(nc.vector.tensor_reduce(slot_e[:], past[:], AX.X, ALU.add))
            nc.vector.tensor_scalar(slot_exp[:], slot_e[:], float(NE - 1), None, ALU.min).then_inc(exp_table, 1)
            dve.wait_ge(rowhot_used, R)
            then(nc.vector.tensor_copy(src_tile[:], bank[7][:, 288:320]))
            nc.vector.scalar_tensor_tensor(out=src_rows[:], in0=src_tile[:], scalar=float(P), in1=bank[7][:, 256:288],
                                           op0=ALU.mult, op1=ALU.add).then_inc(src_ready, 1)
            pair_mul(6)
            pair_mul(7)

            def out_h(s, m):
                dve.wait_ge(h_turned, s + 1)
                ge(dve, y_done, s - 1)
                nc.vector.tensor_copy(hT[m % 2][:], bank[2 + m % 2][:, 0:P]).then_inc(hT_out, 1)

            def mul_h(s, m):
                dve.wait_ge(silu_done, s + 1)
                ge(dve, h_turned, s - 1)
                nc.vector.tensor_tensor(hh[m % 2][:], bank[m % 2][:, FE:2 * FE], sg[m % 2][:], ALU.mult)\
                    .then_inc(h_ready, 1)

            def weights_lo(s, m, e, a):
                dve.wait_ge(w_hi, s + 1)
                nc.vector.tensor_tensor(wsp[m % 2][:, 1, a:a + 2, :], raw_gu(e, a),
                                        wsp[m % 2][:, 0, a:a + 2, :].bitcast(F32), ALU.subtract).then_inc(w_lo, 1)

            def tokens_lo(s, m):
                dve.wait_ge(gT_hi, s + 1)
                nc.vector.tensor_tensor(gT[m % 2][:, 1], bank[4 + m % 2][:].rearrange("p (c t) -> p c t", c=C),
                                        gT[m % 2][:, 0].bitcast(F32), ALU.subtract).then_inc(gT_out, 1)

            def step(s, m):
                more = not (isinstance(s, int) and s + 1 >= NS)
                if more:
                    e = expert_of(dve, s + 1)
                    weights_lo(s + 1, m + 1, e, 0)
                if m:
                    out_h(s - 1, m - 1)
                if more:
                    tokens_lo(s + 1, m + 1)
                mul_h(s, m)
                if more:
                    weights_lo(s + 1, m + 1, e, 2)

            dve.wait_ge(exp_table, 1)
            e = expert_of(dve, 0)
            weights_lo(0, 0, e, 0)
            for j in range(2):
                add_shared(24, j, j).then_inc(ring_out, 1)
            tokens_lo(0, 0)
            weights_lo(0, 0, e, 2)
            slot_steps(dve, step)
            out_h(NS - 1, NS - 1)

            def combine(t):
                for k in range(TOPK):
                    n = t * TOPK + k
                    dve.wait_ge(back[n % NG], 16 * (n // NG + 1))
                    if k:
                        dve.wait_ge(back_used, n)
                    last = nc.vector.scalar_tensor_tensor(out=xs[:, t, :], in0=grow[n % NG][:],
                                                          scalar=wtop[:, t, k:k + 1], in1=xs[:, t, :],
                                                          op0=ALU.mult, op1=ALU.add)
                    last.then_inc(back_used, 1)

            shared_before = {0: 2, 1: 3, 3: 4, 4: 5, 6: 6}
            for t in range(NT):
                if t in shared_before:
                    j = shared_before[t]
                    add_shared(24, j, j).then_inc(ring_out, 1)
                if 2 <= t < NT - 1:
                    dve.wait_ge(ring_out, 24 + t + 1)
                combine(t)
            dve.wait_ge(back_used, TOPK * NT)
            add_shared(24, NT - 1, NT - 1).then_inc(ring_out, 1)


_OUT = ((16, 64, 512), 'float32')


def kernel(x, ctx_4096, L0_xattn_Wq, L0_xattn_bq, L0_xattn_Wk, L0_xattn_bk, L0_ffn_gate_w, L0_ffn_w_gate_up,
           L0_ffn_w_down, L0_ffn_shared_w_gate_up, L0_ffn_shared_w_down):
    import numpy as np
    import concourse.bacc as bacc
    from concourse.bass_utils import run_bass_kernel_spmd

    def feature_chunks(a):
        a = np.asarray(a)
        a = a.reshape(a.shape[:-1] + (a.shape[-1] // 128, 128))
        return np.ascontiguousarray(np.moveaxis(a, (-1, -2), (0, 1)))

    def token_tiles(a):
        a = np.asarray(a).reshape(8, 128, 512)
        return np.ascontiguousarray(a.transpose(1, 0, 2))

    gu = np.asarray(L0_ffn_w_gate_up)
    arrays = {
        "x": token_tiles(x),
        "ctx_t": feature_chunks(np.asarray(ctx_4096).reshape(1024, 512)),
        "ctx_n": token_tiles(ctx_4096),
        "wq_t": feature_chunks(L0_xattn_Wq),
        "wk_t": feature_chunks(L0_xattn_Wk),
        "bq": feature_chunks(L0_xattn_bq),
        "bk": feature_chunks(L0_xattn_bk),
        "gate_t": feature_chunks(L0_ffn_gate_w),
        "moe_gu_t": np.ascontiguousarray(feature_chunks(gu).transpose(0, 2, 1, 3)),
        "moe_dn_t": np.ascontiguousarray(np.asarray(L0_ffn_w_down).transpose(2, 0, 1)),
        "sh_gu_t": feature_chunks(L0_ffn_shared_w_gate_up),
        "sh_dn_t": feature_chunks(L0_ffn_shared_w_down),
    }
    nc = bacc.Bacc("TRN2", target_bir_lowering=False, num_devices=1)
    args = [nc.dram_tensor(n, a.shape, mybir.dt.from_np(a.dtype), kind="ExternalInput").ap()
            for n, a in arrays.items()]
    out = nc.dram_tensor("out", (128, 8, 512), F32, kind="ExternalOutput").ap()
    xattn_moe(nc, *args, out)
    r = run_bass_kernel_spmd(nc, [arrays], core_ids=[0])
    got = r.results[0]["out"]
    return np.ascontiguousarray(got.transpose(1, 0, 2)).reshape(_OUT[0])
```

```python
from contextlib import ExitStack

import concourse.bass as bass
from concourse import mybir

F32 = mybir.dt.float32
F32R = mybir.dt.float32r
BF16 = mybir.dt.bfloat16
I32 = mybir.dt.int32
U32 = mybir.dt.uint32
ALU = mybir.AluOpType
ACT = mybir.ActivationFunctionType
AX = mybir.AxisListType

P = 128


def xattn_moe(nc, x, ctx_t, ctx_n, wq_t, wk_t, bq, bk, gate_t, moe_gu_t, moe_dn_t, sh_gu_t, sh_dn_t, out):
    _, NT, D = x.shape
    T = NT * P
    C = D // P
    SEQ = 64
    NE = gate_t.shape[2]
    TOPK = 2
    FE = moe_dn_t.shape[0]
    SC = sh_dn_t.shape[1]
    HALF = NT // 2
    HW = HALF * P
    NS = T * TOPK // P + NE - 1
    SCALE = float(D) ** -0.5
    EPS = 1e-5

    xn_dram = nc.dram_tensor("xn_dram", (T, D), F32, kind="Internal").ap()
    y_dram = nc.dram_tensor("y_dram", (NS * P, D), F32, kind="Internal").ap()

    with ExitStack() as ctx:
        def sb(name, shape, dt=F32):
            return ctx.enter_context(nc.sbuf_tensor(name, shape, dt))

        def sem(name):
            return ctx.enter_context(nc.semaphore(name))

        bank = [ctx.enter_context(nc.psum_tensor(f"bank{i}", [P, 512], F32)) for i in range(8)]

        KB = 1024
        base = (nc.sbuf_base + 63) // 64 * 64
        ctx.enter_context(nc.sbuf_tensor("fence", [P, (base - nc.sbuf_base + 192 * KB) // 4 + 8], F32))

        def at(name, kb, shape, dt=F32):
            return nc.alloc_sbuf_tensor_at(name, shape, dt, offset=base + int(kb * KB))

        GUW = C * 2 * FE
        moe_gu = at("moe_gu", 0, [P, NE * GUW])
        moe_dn = at("moe_dn", 64, [P, NE * D])
        ctxN = at("ctxN", 0, [P, NT, D])
        ctx0T = at("ctx0T", 0, [P, 2, C, HW], F32R)
        kT = at("kT", 16, [P, C, T])
        ctx1T = at("ctx1T", 32, [P, 2, C, HW], F32R)
        qT = at("qT", 32, [P, C, T])
        wqT = at("wqT", 48, [P, 2, C, D], F32R)
        wk_raw = at("wk_raw", 64, [P, C, D])
        wq_raw = at("wq_raw", 72, [P, C, D])
        sh_raw = at("sh_raw", 64, [P, SC, 2, C, P])
        wkT = at("wkT", 96, [P, 2, C, D], F32R)
        ctx_raw = [at(f"ctx_raw{h}", 112 + 8 * h, [P, C, HW]) for h in range(2)]
        sh_gu = [at(f"sh_gu{i}", 96 + 16 * i, [P, SC, 2, C, P], F32R) for i in range(2)]
        lgT = at("lgT", 0, [2 * NE, 2, HW])
        sh_dn = at("sh_dn", 128, [P, SC, D])
        sh_dn2 = [at("sh_dn_hi", 120, [P, SC, D], F32R), at("sh_dn_lo", 128, [P, SC, D], F32R)]
        xs = at("xs", 136, [P, NT, D])
        xn = at("xn", 152, [P, NT, D])
        xT = [at("xT0", 80, [P, 2, C, HW], F32R), at("xT1", 168, [P, 2, C, HW], F32R)]
        NG = 4
        grow = [at(f"grow{i}", 152 + 2 * i, [P, D]) for i in range(NG)]
        rowhot = [at(f"rowhot{n}", 152 + n / 4, [P, P], BF16) for n in range(NT * TOPK)]
        slothot = at("slothot", 156, [P, NT * TOPK, 2, 32], BF16)
        past = at("past", 158, [1, 32, NE])
        wsp = [at(f"wsp{i}", 96 + 16 * i, [P, 2, C, 2 * FE], F32R) for i in range(2)]
        gT = [at(f"gT{i}", 104 + 4 * i, [P, 2, C, P], F32R) for i in range(2)]
        sg = [at(f"sg{i}", 168 + i / 2, [P, FE]) for i in range(2)]
        hh = [at(f"hh{i}", 169 + i / 2, [P, FE]) for i in range(2)]
        hT = [at(f"hT{i}", 170 + i / 2, [P, P]) for i in range(2)]
        ys = [at(f"ys{i}", 172 + 2 * i, [P, D]) for i in range(2)]
        hsT = [at("hsT0", 184, [P, SC, HW]), at("hsT1", 160, [P, SC, HW])]
        hsT_lo = [at("hsT_lo0", 184, [P, SC, HW], F32R), at("hsT_lo1", 160, [P, SC, HW], F32R)]
        hsT_hi = [at(f"hsT_hi{t}", (176, 96)[t // HALF] + 2 * (t % HALF), [P, SC, P], F32R) for t in range(NT)]
        NB = 8
        gback = [at(f"gback{i}", (152, 104)[i // NG] + 2 * (i % NG), [P, D]) for i in range(NB)]
        gate = sb("gate", [P, C, NE])
        gate2 = sb("gate2", [P, C, 2, NE], F32R)
        bqs = sb("bqs", [P, C])
        bks = sb("bks", [P, C])
        ident = sb("ident", [P, P])
        before = sb("before", [P, P], BF16)
        ones = sb("ones", [P, P], BF16)
        iota_f = sb("iota_f", [P, P])
        tile_no = sb("tile_no", [P, NT])
        tile_row = sb("tile_row", [P, 1])
        steps128 = sb("steps128", [P, 8])
        lower_e = sb("lower_e", [P, NE, NE])
        neg_half = sb("neg_half", [P, 2 * NT])
        stats = sb("stats", [P, NT, 6])
        meanvar = sb("meanvar", [P, NT, 2])
        vareps = sb("vareps", [P, NT])
        rstd = sb("rstd", [P, NT])
        neg_mean = sb("neg_mean", [P, NT])
        shift = sb("shift", [P, NT])
        E = [hsT[0][:, h, :].rearrange("p (t k) -> p t k", t=HALF) for h in range(2)]
        ET = hsT[0][:, 2, :].rearrange("p (t k) -> p t k", t=HALF)
        smax = sb("smax", [P, NT])
        ssum = sb("ssum", [P, NT])
        rsum = sb("rsum", [P, NT])
        silu_s = [sb(f"silu_s{i}", [P, HW]) for i in range(2)]
        rmax = sb("rmax", [P, NT])
        prob = sb("prob", [P, NT, NE])
        psm = sb("psm", [P, NT])
        prs = sb("prs", [P, NT])
        top = sb("top", [P, NT, 8])
        topi = sb("topi", [P, NT, 8], U32)
        topf = sb("topf", [P, NT, TOPK])
        wsum = sb("wsum", [P, NT])
        wrec = sb("wrec", [P, NT])
        wtop = sb("wtop", [P, NT, TOPK])
        pick = [sb(f"pick{k}", [P, NT, NE]) for k in range(TOPK)]
        picked = sb("picked", [P, NT, NE], BF16)
        over = sb("over", [P, NE, 8])
        ntile = sb("ntile", [P, NE])
        prod_e = sb("prod_e", [P, NE, NE])
        first = sb("first", [P, NE])
        place = sb("place", [P, NT, NE])
        placed = [sb(f"placed{k}", [P, NT, NE]) for k in range(TOPK)]
        rows = sb("rows", [P, NT, TOPK])
        rows_i = sb("rows_i", [P, NT, TOPK], I32)
        rows_u = sb("rows_u", [P, NT, TOPK], U32)
        slot_i = sb("slot_i", [P, NT, TOPK], I32)
        slot_f = sb("slot_f", [P, NT, TOPK])
        inrow = sb("inrow", [P, NT, TOPK])
        last_e = sb("last_e", [1, NE])
        slot_e = sb("slot_e", [1, 32])
        slot_exp = sb("slot_exp", [1, 32], I32)
        src_tile = sb("src_tile", [P, 32])
        src_rows = sb("src_rows", [P, 32], U32)

        ld = {n: sem(f"ld_{n}") for n in (
            "small", "key0", "key1", "key2", "key3", "ctx1", "x0", "x1", "wq", "ctxN", "shgu", "shdn", "dn0", "dn1", "gu0", "gu1", "gu2", "gu3")}
        split_hi = {n: sem(f"hi_{n}") for n in ("key", "ctx1", "wq", "shgu", "gate")}
        split_lo = {n: sem(f"lo_{n}") for n in ("key", "ctx1a", "ctx1b", "wq", "shgu", "gate")}
        warm_ready = sem("warm_ready")
        const_step = sem("const_step")
        const_ready = sem("const_ready")
        dve_step = sem("dve_step")
        zeroed = sem("zeroed")
        var_ready = sem("var_ready")
        rstd_ready = sem("rstd_ready")
        shift_ready = sem("shift_ready")
        xn_act = sem("xn_act")
        xn_ready = sem("xn_ready")
        xn_stored = sem("xn_stored")
        proj_done = sem("proj_done")
        proj_out = sem("proj_out")
        ring_done = sem("ring_done")
        ring_hi = sem("ring_hi")
        ring_out = sem("ring_out")
        score_done = sem("score_done")
        shifted = sem("shifted")
        exp_done = sem("exp_done")
        exp_half = sem("exp_half")
        shift_half = sem("shift_half")
        et_done = sem("et_done")
        et_out = sem("et_out")
        logitT_done = sem("logitT_done")
        logitT_out = sem("logitT_out")
        logit_done = sem("logit_done")
        rshift = sem("rshift")
        rexp = sem("rexp")
        gate_done = sem("gate_done")
        up_done = sem("up_done")
        pair_silu = sem("pair_silu")
        pair_out = sem("pair_out")
        picked_ready = sem("picked_ready")
        count_done = sem("count_done")
        exp_table = sem("exp_table")
        slothot_ready = sem("slothot_ready")
        rowhot_ready = sem("rowhot_ready")
        map_done = sem("map_done")
        src_ready = sem("src_ready")
        rows_ready = sem("rows_ready")
        gathered = [sem(f"gathered{i}") for i in range(NG)]
        turned = sem("turned")
        w_hi = sem("w_hi")
        w_lo = sem("w_lo")
        gT_hi = sem("gT_hi")
        gT_out = sem("gT_out")
        gu_done = sem("gu_done")
        silu_done = sem("silu_done")
        h_ready = sem("h_ready")
        h_turned = sem("h_turned")
        hT_out = sem("hT_out")
        y_done = sem("y_done")
        y_out = sem("y_out")
        y_stored = [sem(f"y_stored{i}") for i in range(2)]
        back = [sem(f"back{i}") for i in range(NB)]
        back_used = sem("back_used")
        dn_hi = sem("dn_hi")
        dn_lo = sem("dn_lo")
        hs_hi = sem("hs_hi")
        hs_lo = [sem(f"hs_lo{h}") for h in range(2)]
        stored = sem("stored")

        LOOP0 = 4
        UNROLL = 2 * NG
        LOOPN = (NS - 1 - LOOP0) // UNROLL

        def slot_steps(eng, step):
            for s in range(LOOP0):
                step(s, s)
            with eng.Fori(0, LOOPN) as i:
                for u in range(UNROLL):
                    step(UNROLL * i + (LOOP0 + u), LOOP0 + u)
            for s in range(LOOP0 + UNROLL * LOOPN, NS):
                step(s, s)

        def ge(eng, s, value):
            if not isinstance(value, int) or value > 0:
                eng.wait_ge(s, value)

        def expert_of(eng, s):
            src = slot_exp[0:1, s:s + 1] if isinstance(s, int) else slot_exp[0:1, bass.ds(s, 1)]
            return eng.value_load(src, min_val=0, max_val=NE - 1)

        def raw_gu(e, a):
            return moe_gu[:, bass.ds(e * GUW + a * 2 * FE, 4 * FE)].rearrange("p (c i) -> p c i", c=2)

        RING = [4, 5] * 4 + [4, 5, 7, 4] + [5, 4, 0, 1] + [5, 4, 7, 5] + [4, 5, 6, 7] + [4, 5] * 4

        def ring_before(m):
            return max((k + 1 for k in range(m) if RING[k] == RING[m]), default=0)

        block = ctx.enter_context(nc.Block())

        @block.sync
        def _(sp):
            def load(name, dst, src):
                sp.dma_start(dst, src).then_inc(ld[name], 16)

            for c in range(C):
                load(f"key{c}", wk_raw[:, c], wk_t[:, c])
                load(f"key{c}", ctx_raw[0][:, c], ctx_t[:, c, 0:HW])
            load("x0", xs[:, 0:HALF, :], x[:, 0:HALF, :])
            load("small", bqs[:], bq)
            load("small", bks[:], bk)
            load("small", gate[:], gate_t)
            load("ctx1", ctx_raw[1][:], ctx_t[:, :, HW:T])
            load("wq", wq_raw[:], wq_t)
            load("x1", xs[:, HALF:NT, :], x[:, HALF:NT, :])
            load("shdn", sh_dn[:], sh_dn_t)
            sp.wait_ge(proj_done, 4)
            load("ctxN", ctxN[:], ctx_n)
            sp.wait_ge(split_lo["key"], 2 * C)
            sp.wait_ge(split_lo["wq"], 1)
            load("shgu", sh_raw[:], sh_gu_t)
            gu_flat = moe_gu_t.rearrange("p e c i -> p (e c i)")
            dn_flat = moe_dn_t.rearrange("p e d -> p (e d)")
            sp.wait_ge(proj_done, 16)
            load("gu3", moe_gu[:, 12288:16384], gu_flat[:, 12288:16384])
            sp.wait_ge(split_lo["shgu"], 2)
            load("dn0", moe_dn[:, 0:4096], dn_flat[:, 0:4096])
            sp.wait_ge(score_done, 2)
            load("gu1", moe_gu[:, 4096:8192], gu_flat[:, 4096:8192])
            load("gu2", moe_gu[:, 8192:12288], gu_flat[:, 8192:12288])
            for h in range(2):
                sp.wait_ge(xn_ready, NT + 2 * (h + 1))
                sp.wait_ge(xn_act, 2 * (h + 1))
                sp.dma_start(xn_dram[h * HW:(h + 1) * HW, :].rearrange("(t p) d -> p t d", p=P),
                             xn[:, h * HALF:(h + 1) * HALF, :]).then_inc(xn_stored, 16)

            def store(s, m):
                sp.wait_ge(y_out, s + 1)
                dst = y_dram[bass.ds(s * P, P), :] if not isinstance(s, int) else y_dram[s * P:(s + 1) * P, :]
                sp.dma_start(dst, ys[m % 2][:]).then_inc(y_stored[m % 2], 16)

            sp.wait_ge(logit_done, 2)
            load("gu0", moe_gu[:, 0:4096], gu_flat[:, 0:4096])
            sp.wait_ge(up_done, SC)
            load("dn1", moe_dn[:, 4096:8192], dn_flat[:, 4096:8192])
            slot_steps(sp, store)
            for t in range(NT):
                sp.wait_ge(back_used, TOPK * (t + 1))
                sp.dma_start(out[:, t, :], xs[:, t, :]).then_inc(stored, 16)
            sp.wait_ge(stored, 16 * NT)

        @block.gpsimd
        def _(pool):
            steps = [0]

            def then(ins):
                steps[0] += 1
                ins.then_inc(const_step, 1)
                pool.wait_ge(const_step, steps[0])

            then(nc.gpsimd.memset(ident[:], 0.0))
            nc.gpsimd.affine_select(out=ident[:], in_=ident[:], compare_op=ALU.not_equal, fill=1.0, base=0,
                                    pattern=[[-1, P]], channel_multiplier=1).then_inc(const_ready, 1)
            for h in range(2):
                then(nc.gpsimd.memset(E[h], 0.0))
            nc.gpsimd.memset(ones[:], 1.0).then_inc(const_ready, 1)

            def rsqrt(n):
                a = 2 * (n % HALF)
                b = a + 2
                pool.wait_ge(var_ready, n + 1)
                nc.gpsimd.tensor_tensor(out=rstd[:, a:b], in0=vareps[:, a:b], in1=neg_half[:, a:b],
                                        op=ALU.pow).then_inc(rstd_ready, 1)

            pool.wait_ge(const_ready, 3)

            def lo_of(name, n, lo, raw, hi, part=""):
                pool.wait_ge(split_hi[name], n)
                nc.gpsimd.tensor_tensor(out=lo, in0=raw, in1=hi.bitcast(F32), op=ALU.subtract)\
                    .then_inc(split_lo[name + part], 1)

            rsqrt(0)
            rsqrt(1)
            for c in range(2):
                lo_of("ctx1", 1, ctx1T[:, 1, c], ctx_raw[1][:, c], ctx1T[:, 0, c], "a")
            lo_of("wq", 1, wqT[:, 1], wq_raw[:], wqT[:, 0])
            lo_of("gate", 1, gate2[:, :, 1], gate[:], gate2[:, :, 0])
            rsqrt(2)
            rsqrt(3)
            then(nc.gpsimd.memset(before[:], 1.0))
            nc.gpsimd.affine_select(out=before[:], in_=before[:], compare_op=ALU.is_gt, fill=0.0, base=0,
                                    pattern=[[1, P]], channel_multiplier=-1).then_inc(const_ready, 1)
            nc.gpsimd.iota(iota_f[:], pattern=[[1, P]], base=0, channel_multiplier=0,
                           allow_small_or_imprecise_dtypes=True).then_inc(const_ready, 1)
            nc.gpsimd.iota(tile_no[:], pattern=[[1, NT]], base=0, channel_multiplier=0,
                           allow_small_or_imprecise_dtypes=True).then_inc(const_ready, 1)
            nc.gpsimd.iota(tile_row[:], pattern=[[0, 1]], base=0, channel_multiplier=1,
                           allow_small_or_imprecise_dtypes=True).then_inc(const_ready, 1)
            nc.gpsimd.iota(steps128[:], pattern=[[P, 8]], base=0, channel_multiplier=0,
                           allow_small_or_imprecise_dtypes=True).then_inc(const_ready, 1)
            then(nc.gpsimd.memset(lower_e[:], 1.0))
            nc.gpsimd.affine_select(out=lower_e[:], in_=lower_e[:], compare_op=ALU.is_gt, fill=0.0, base=0,
                                    pattern=[[1, NE], [-1, NE]], channel_multiplier=0).then_inc(const_ready, 1)
            for i in range(2):
                lo_of("shgu", i + 1, sh_gu[1][:, 2 * i:2 * i + 2], sh_raw[:, 2 * i:2 * i + 2], sh_gu[0][:, 2 * i:2 * i + 2])
            for n in range(HALF, 2 * HALF):
                rsqrt(n)
                if n % 2 == 0:
                    t = slice(2 * (n - HALF), 2 * (n - HALF) + 2)
                    nc.gpsimd.tensor_scalar(neg_mean[:, t], meanvar[:, t, 0], -1.0, None, ALU.mult)\
                        .then_inc(shift_ready, 1)
                    pool.wait_ge(shift_ready, n - HALF + 1)
                    pool.wait_ge(rstd_ready, n + 1)
                    nc.gpsimd.tensor_tensor(out=shift[:, t], in0=neg_mean[:, t], in1=rstd[:, t], op=ALU.mult)\
                        .then_inc(shift_ready, 1)
            pool.wait_ge(src_ready, 1)
            pool.wait_ge(xn_stored, 32)
            for s in range(NS):
                ge(pool, turned, s - NG + 1)
                if s == NG - 1:
                    pool.wait_ge(exp_table, 1)
                nc.gpsimd.indirect_dma_start(
                    out=grow[s % NG][:], out_offset=None, in_=xn_dram,
                    in_offset=bass.IndirectOffsetOnAxis(ap=src_rows[:, s:s + 1], axis=0),
                ).then_inc(gathered[s % NG], 16)
                if NG <= s < NG + SC:
                    c = s - NG
                    pool.wait_ge(dn_hi, c + 1)
                    nc.gpsimd.tensor_tensor(out=sh_dn2[1][:, c], in0=sh_dn[:, c], in1=sh_dn2[0][:, c].bitcast(F32),
                                            op=ALU.subtract).then_inc(dn_lo, 1)
            for t in range(HALF):
                pool.wait_ge(hs_hi, t + 1)
                r = slice(t * P, (t + 1) * P)
                nc.gpsimd.tensor_tensor(out=hsT_lo[0][:, :, r], in0=hsT[0][:, :, r], in1=hsT_hi[t][:].bitcast(F32),
                                        op=ALU.subtract).then_inc(hs_lo[0], 1)
            pool.wait_ge(turned, NS)
            pool.wait_ge(y_stored[0], 16 * ((NS + 1) // 2))
            pool.wait_ge(y_stored[1], 16 * (NS // 2))
            pool.wait_ge(rows_ready, 1)
            for n in range(NT * TOPK):
                t, k = n // TOPK, n % TOPK
                ge(pool, back_used, n - NB + 1)
                nc.gpsimd.indirect_dma_start(
                    out=gback[n % NB][:], out_offset=None, in_=y_dram,
                    in_offset=bass.IndirectOffsetOnAxis(ap=rows_u[:, t, k:k + 1], axis=0),
                ).then_inc(back[n % NB], 16)

        @block.tensor
        def _(pe):
            def mm(o, w, m, start, stop):
                return nc.tensor.matmul(o, w, m, start=start, stop=stop)

            def mm3(o, w, m, start, stop):
                mm(o, w(0), m(0), start, False)
                mm(o, w(0), m(1), False, False)
                return mm(o, w(1), m(0), False, stop)

            def project_first():
                for c in range(C):
                    pe.wait_ge(split_lo["key"], 2 * (c + 1))
                    for o in range(C):
                        last = mm3(bank[o][:], lambda i: wkT[:, i, c, o * P:(o + 1) * P], lambda i: ctx0T[:, i, c, :],
                                   c == 0, c == C - 1)
                        if c == C - 1:
                            last.then_inc(proj_done, 1)

            def project(n, w, mov, o):
                pe.wait_ge(proj_out, n - 3)
                for c in range(C):
                    if n == 4:
                        pe.wait_ge(split_lo["ctx1a" if c < 2 else "ctx1b"], c + 1 if c < 2 else 1)
                    last = mm3(bank[n % 4][:], lambda i: w[:, i, c, o * P:(o + 1) * P], lambda i: mov[:, i, c, :],
                               c == 0, c == C - 1)
                last.then_inc(proj_done, 1)

            def ring(m):
                ge(pe, ring_out, ring_before(m))
                return bank[RING[m]]

            def turn_xn(m, h, xn_before, js):
                for j in js:
                    t = h * HALF + j
                    if xn_before == 0:
                        pe.wait_ge(xn_ready, t + 1)
                    elif j < 2:
                        pe.wait_ge(xn_act, 2 * h + j + 1)
                    else:
                        pe.wait_ge(xn_ready, xn_before + 2 * h + j - 1)
                    b = ring(m + j)
                    for c in range(C):
                        last = nc.tensor.transpose(b[:, c * P:(c + 1) * P], xn[:, t, c * P:(c + 1) * P], ident[:])
                    last.then_inc(ring_done, 1)

            def scores(h, js):
                pe.wait_ge(proj_out, 12 + 4 * h)
                if h:
                    pe.wait_ge(shifted, 1)
                for j in js:
                    a = (h * HALF + j) * P
                    for c in range(C):
                        last = mm(bank[6][:, j * P:(j + 1) * P], qT[:, c, a:a + P], kT[:, c, a:a + P],
                                  c == 0, c == C - 1)
                if HALF - 1 in js:
                    last.then_inc(score_done, 1)

            def turn_exp(h):
                pe.wait_ge(exp_done, h + 1)
                if h:
                    pe.wait_ge(et_out, 1)
                for j in range(HALF):
                    last = nc.tensor.transpose(bank[7][:, j * P:(j + 1) * P], E[h][:, j, :], ident[:])
                last.then_inc(et_done, 1)

            def attend(m, h, js):
                pe.wait_ge(et_out, h + 1)
                pe.wait_ge(ld["ctxN"], 16)
                for j in js:
                    b = ring(m + j)
                    mm(b[:], ET[:, j, :], ctxN[:, h * HALF + j, :], True, True).then_inc(ring_done, 1)

            def shared(h, j, g):
                n = h * SC + j
                if n >= 2:
                    pe.wait_ge(pair_out, n - 1)
                for c in range(C):
                    last = mm3(bank[2 * (n % 2) + g][:], lambda i: sh_gu[i][:, j, g, c, :],
                               lambda i: xT[h][:, i, c, :], c == 0, c == C - 1)
                last.then_inc((gate_done, up_done)[g], 1)

            def logits(h):
                b = bank[6 + h]
                for c in range(C):
                    for i in range(2):
                        last = mm(b[0:2 * NE, :], gate2[:, c].rearrange("p i e -> p (i e)"), xT[h][:, i, c, :],
                                  c == 0 and i == 0, c == C - 1 and i == 1)
                last.then_inc(logitT_done, 1)

            def turn_logits(h):
                pe.wait_ge(logitT_out, h + 1)
                for j in range(HALF):
                    t = h * HALF + j
                    last = nc.tensor.transpose(bank[6][:, 2 * t * NE:2 * (t + 1) * NE], lgT[:, h, j * P:(j + 1) * P],
                                               ident[0:2 * NE, 0:2 * NE])
                last.then_inc(logit_done, 1)

            def shared_down(t, chunks=range(SC)):
                pe.wait_ge(hs_lo[t // HALF], t % HALF + 1)
                b = ring(24 + t)
                r = slice(t % HALF * P, (t % HALF + 1) * P)
                hs = (hsT_hi[t], hsT_lo[t // HALF][:, :, r])
                for c in chunks:
                    last = mm3(b[:], lambda i: hs[i][:, c, :], lambda i: sh_dn2[i][:, c, :], c == 0, c == SC - 1)
                if SC - 1 in chunks:
                    last.then_inc(ring_done, 1)

            pe.wait_ge(warm_ready, 1)
            for _ in range(5):
                mm(bank[7][:, 0:256], silu_s[0][:, 0:P], silu_s[0][:, 0:256], True, True)

            project_first()
            pe.wait_ge(const_ready, 3)
            turn_xn(0, 0, 0, (0, 1))
            project(4, wkT, ctx1T, 0)
            turn_xn(0, 0, 0, (2, 3))
            for o in range(1, C):
                project(4 + o, wkT, ctx1T, o)
            pe.wait_ge(split_lo["wq"], 1)
            pe.wait_ge(ring_out, 4)
            project(8, wqT, xT[0], 0)
            turn_xn(4, 1, 0, (0, 1))
            project(9, wqT, xT[0], 1)
            turn_xn(4, 1, 0, (2, 3))
            project(10, wqT, xT[0], 2)
            project(11, wqT, xT[0], 3)
            pe.wait_ge(ring_out, 8)
            project(12, wqT, xT[1], 0)
            scores(0, range(HALF))
            project(13, wqT, xT[1], 1)
            turn_exp(0)
            project(14, wqT, xT[1], 2)
            attend(8, 0, range(HALF))
            project(15, wqT, xT[1], 3)
            turn_xn(12, 0, NT, (0, 1))
            scores(1, (0, 1))
            turn_xn(12, 0, NT, (2, 3))
            scores(1, (2, 3))
            pe.wait_ge(ring_out, 16)
            pe.wait_ge(split_lo["shgu"], 2)
            shared(0, 0, 0)
            turn_exp(1)
            shared(0, 0, 1)
            attend(16, 1, range(HALF))
            pe.wait_ge(split_lo["gate"], 1)
            pe.wait_ge(shifted, 2)
            logits(0)
            shared(0, 1, 0)
            shared(0, 1, 1)
            pe.wait_ge(logitT_out, 1)
            turn_xn(20, 1, NT, range(HALF))
            shared(0, 2, 0)
            pe.wait_ge(ring_out, 24)
            logits(1)
            turn_logits(0)
            shared(0, 2, 1)
            turn_logits(1)
            shared(0, 3, 0)
            shared(0, 3, 1)
            shared(1, 0, 0)
            pe.wait_ge(picked_ready, 1)
            pe.wait_ge(const_ready, 9)
            W = NT * NE
            pk = picked[:].rearrange("p t e -> p (t e)")
            mm(bank[7][:, 0:W], before[:], pk, True, False)
            for d in range(1, NT):
                mm(bank[7][:, d * NE:W], ones[:], pk[:, 0:W - d * NE], False, d == NT - 1)
            for t in range(NT):
                last = mm(bank[6][:, 256:256 + NE], ones[:], picked[:, t, :], t == 0, t == NT - 1)
            last.then_inc(count_done, 1)
            shared(1, 0, 1)
            shared(1, 1, 0)
            shared(1, 1, 1)
            shared(1, 2, 0)
            pe.wait_ge(slothot_ready, 2)
            for n in range(NT * TOPK):
                pe.wait_ge(rowhot_ready, n + 1)
                last = mm(bank[7][:, 256:320], rowhot[n][:], slothot[:, n].rearrange("p a s -> p (a s)"), n == 0,
                          n == NT * TOPK - 1)
            last.then_inc(map_done, 1)
            shared(1, 2, 1)

            pe.wait_ge(exp_table, 1)
            for n in ("dn0", "dn1", "gu0", "gu1", "gu2", "gu3"):
                pe.wait_ge(ld[n], 16)

            def turn(s, m):
                g = m % NG
                pe.wait_ge(gathered[g], 16 * ((s - g) // NG + 1) if isinstance(s, int) else loop_turn(s, m))
                ge(pe, gT_out, s - 1)
                b = bank[4 + m % 2]
                for c in range(C):
                    last = nc.tensor.transpose(b[:, c * P:(c + 1) * P], grow[g][:, c * P:(c + 1) * P], ident[:])
                last.then_inc(turned, 1)

            def gate_up(s, m, chunks):
                if 0 in chunks:
                    pe.wait_ge(gT_out, s + 1)
                    ge(pe, h_ready, s - 1)
                pe.wait_ge(w_lo, 2 * s + (1 if 0 in chunks else 2))
                for c in chunks:
                    last = mm3(bank[m % 2][:, 0:2 * FE], lambda i: gT[m % 2][:, i, c, :],
                               lambda i: wsp[m % 2][:, i, c, :], c == 0, c == C - 1)
                if C - 1 in chunks:
                    last.then_inc(gu_done, 1)

            def turn_h(s, m):
                if isinstance(s, int) and s == 0:
                    pe.wait_ge(pair_out, 2 * SC)
                pe.wait_ge(h_ready, s + 1)
                ge(pe, hT_out, s - 1)
                nc.tensor.transpose(bank[2 + m % 2][:, 0:P], hh[m % 2][:], ident[:]).then_inc(h_turned, 1)

            def down(s, m, e):
                pe.wait_ge(hT_out, s + 1)
                ge(pe, y_out, s - 1)
                mm(bank[6 + m % 2][:], hT[m % 2][:], moe_dn[:, bass.ds(e * D, D)], True, True).then_inc(y_done, 1)

            counter = [None]

            def loop_turn(s, m):
                return 16 * (UNROLL // NG) * counter[0] + 16 * (m // NG + 1)

            def step(s, m):
                more = not (isinstance(s, int) and s + 1 >= NS)
                if m:
                    e = expert_of(pe, s - 1)
                if more:
                    turn(s + 1, m + 1)
                gate_up(s, m, (0, 1))
                if m:
                    turn_h(s - 1, m - 1)
                gate_up(s, m, (2, 3))
                if m:
                    down(s - 1, m - 1, e)

            shared(1, 3, 0)
            turn(0, 0)
            shared(1, 3, 1)
            pe.wait_ge(pair_out, 2 * SC - 1)
            for s in range(LOOP0):
                step(s, s)
            with pe.Fori(0, LOOPN) as i:
                counter[0] = i
                for u in range(UNROLL):
                    step(UNROLL * i + (LOOP0 + u), LOOP0 + u)
            for s in range(LOOP0 + UNROLL * LOOPN, NS):
                step(s, s)
            pe.wait_ge(dn_lo, SC)
            shared_down(0, (0,))
            turn_h(NS - 1, NS - 1)
            e = expert_of(pe, NS - 1)
            shared_down(0, (1,))
            down(NS - 1, NS - 1, e)
            shared_down(0, (2, 3))
            for t in range(1, NT):
                shared_down(t)

        @block.scalar
        def _(act):
            def proj_evac(n, dst, bias, h, o):
                if n == 0:
                    act.wait_ge(ld["small"], 48)
                act.wait_ge(proj_done, n + 1)
                nc.scalar.activation(dst[:, o, h * HW:(h + 1) * HW], bank[n % 4][:], ACT.Identity,
                                     bias=bias[:, o:o + 1]).then_inc(proj_out, 1)

            def hi_of(name, hi, raw):
                act.wait_ge(ld[name], 16)
                nc.scalar.copy(hi, raw).then_inc(split_hi[name], 1)

            def normalise(h):
                act.wait_ge(shift_ready, 2 * (h + 1))
                for t in (h * HALF, h * HALF + 1):
                    nc.scalar.activation(xn[:, t, :], xs[:, t, :], ACT.Identity, bias=shift[:, t:t + 1],
                                         scale=rstd[:, t:t + 1]).then_inc(xn_act, 1)

            def xT_hi(m, h, js):
                for j in js:
                    act.wait_ge(ring_done, m + j + 1)
                    nc.scalar.copy(xT[h][:, 0, :, j * P:(j + 1) * P],
                                   bank[RING[m + j]][:].rearrange("p (c t) -> p c t", c=C)).then_inc(ring_hi, 1)

            def softmax_exp(h):
                act.wait_ge(shifted, h + 1)
                for b in range(2):
                    r = slice(b * SEQ, (b + 1) * SEQ)
                    last = nc.scalar.activation(E[h][r, :, r], E[h][r, :, r], ACT.Exp, scale=SCALE)
                    if b == 0:
                        last.then_inc(exp_half, 1)
                last.then_inc(exp_done, 1)

            def et_evac(h):
                act.wait_ge(et_done, h + 1)
                if h:
                    act.wait_ge(ring_done, 12)
                nc.scalar.copy(ET, bank[7][:].rearrange("p (t k) -> p t k", t=HALF)).then_inc(et_out, 1)

            def pair_silu_step(n):
                act.wait_ge(gate_done, n + 1)
                if n >= 2:
                    act.wait_ge(pair_out, n - 1)
                nc.scalar.activation(silu_s[n % 2][:], bank[2 * (n % 2)][:], ACT.Silu).then_inc(pair_silu, 1)

            act.wait_ge(warm_ready, 1)
            nc.scalar.mul(neg_half[:], silu_s[0][:, 0:2 * NT], -0.5).then_inc(const_ready, 1)
            for c in range(C):
                act.wait_ge(ld[f"key{c}"], 32)
                nc.scalar.copy(wkT[:, 0, c], wk_raw[:, c]).then_inc(split_hi["key"], 1)
                nc.scalar.copy(ctx0T[:, 0, c], ctx_raw[0][:, c]).then_inc(split_hi["key"], 1)
            for c in (0, 2):
                hi_of("ctx1", ctx1T[:, 0, c:c + 2], ctx_raw[1][:, c:c + 2])
            proj_evac(0, kT, bks, 0, 0)
            nc.scalar.copy(gate2[:, :, 0], gate[:]).then_inc(split_hi["gate"], 1)
            proj_evac(1, kT, bks, 0, 1)
            proj_evac(2, kT, bks, 0, 2)
            proj_evac(3, kT, bks, 0, 3)
            xT_hi(0, 0, (0, 1))
            hi_of("wq", wqT[:, 0], wq_raw[:])
            proj_evac(4, kT, bks, 1, 0)
            xT_hi(0, 0, (2, 3))
            for o in range(1, C):
                proj_evac(4 + o, kT, bks, 1, o)
            proj_evac(8, qT, bqs, 0, 0)
            xT_hi(4, 1, (0, 1))
            proj_evac(9, qT, bqs, 0, 1)
            xT_hi(4, 1, (2, 3))
            proj_evac(10, qT, bqs, 0, 2)
            act.wait_ge(proj_done, 8)
            hi_of("shgu", sh_gu[0][:, 0:2], sh_raw[:, 0:2])
            proj_evac(11, qT, bqs, 0, 3)
            hi_of("shgu", sh_gu[0][:, 2:4], sh_raw[:, 2:4])
            proj_evac(12, qT, bqs, 1, 0)
            softmax_exp(0)
            proj_evac(13, qT, bqs, 1, 1)
            et_evac(0)
            proj_evac(14, qT, bqs, 1, 2)
            normalise(0)
            proj_evac(15, qT, bqs, 1, 3)
            xT_hi(12, 0, (0, 1, 2, 3))
            softmax_exp(1)
            et_evac(1)
            pair_silu_step(0)

            def logitT_evac(h):
                act.wait_ge(logitT_done, h + 1)
                if h == 0:
                    act.wait_ge(ring_done, 20)
                nc.scalar.copy(lgT[:, h, :], bank[6 + h][0:2 * NE, :]).then_inc(logitT_out, 1)

            logitT_evac(0)
            normalise(1)
            pair_silu_step(1)
            xT_hi(20, 1, range(HALF))
            pair_silu_step(2)
            logitT_evac(1)
            act.wait_ge(rshift, 1)
            nc.scalar.activation(prob[:], prob[:], ACT.Exp).then_inc(rexp, 1)
            for n in range(3, 2 * SC - 1):
                pair_silu_step(n)

            act.wait_ge(exp_table, 1)
            for n in ("gu0", "gu1", "gu2", "gu3"):
                act.wait_ge(ld[n], 16)
            act.wait_ge(up_done, 2 * SC - 2)

            def weights_hi(s, m, e):
                ge(act, gu_done, s - 1)
                nc.scalar.copy(wsp[m % 2][:, 0], moe_gu[:, bass.ds(e * GUW, GUW)].rearrange("p (c i) -> p c i", c=C))\
                    .then_inc(w_hi, 1)

            def tokens_hi(s, m):
                act.wait_ge(turned, s + 1)
                ge(act, gu_done, s - 1)
                nc.scalar.copy(gT[m % 2][:, 0], bank[4 + m % 2][:].rearrange("p (c t) -> p c t", c=C))\
                    .then_inc(gT_hi, 1)

            counter = [None]

            def out_y(s, m):
                act.wait_ge(y_done, s + 1)
                if isinstance(s, int):
                    ge(act, y_stored[m % 2], 16 * (s // 2))
                else:
                    act.wait_ge(y_stored[m % 2], 16 * (UNROLL // 2) * counter[0] + 16 * (m // 2))
                nc.scalar.copy(ys[m % 2][:], bank[6 + m % 2][:]).then_inc(y_out, 1)

            def down_hi(c):
                nc.scalar.copy(sh_dn2[0][:, c], sh_dn[:, c]).then_inc(dn_hi, 1)

            def inner_hi(t):
                r = slice(t % HALF * P, (t % HALF + 1) * P)
                nc.scalar.copy(hsT_hi[t][:], hsT[t // HALF][:, :, r]).then_inc(hs_hi, 1)

            def step(s, m):
                if m >= 2:
                    out_y(s - 2, m - 2)
                if not (isinstance(s, int) and s + 1 >= NS):
                    tokens_hi(s + 1, m + 1)
                if not (isinstance(s, int) and s + 2 >= NS):
                    e = expert_of(act, s + 2)
                act.wait_ge(gu_done, s + 1)
                ge(act, h_ready, s - 1)
                nc.scalar.activation(sg[m % 2][:], bank[m % 2][:, 0:FE], ACT.Silu).then_inc(silu_done, 1)
                if not (isinstance(s, int) and s + 2 >= NS):
                    weights_hi(s + 2, m + 2, e)
                if isinstance(s, int):
                    if s == 0:
                        act.wait_ge(ld["shdn"], 16)
                    if s < SC:
                        down_hi(s)
                    if s == NS - 2:
                        act.wait_ge(pair_out, 2 * SC)
                    if s >= NS - 2:
                        for t in range(2):
                            inner_hi(2 * (s - NS + 2) + t)

            weights_hi(0, 0, expert_of(act, 0))
            weights_hi(1, 1, expert_of(act, 1))
            act.wait_ge(up_done, 2 * SC - 1)
            tokens_hi(0, 0)
            pair_silu_step(2 * SC - 1)
            act.wait_ge(up_done, 2 * SC)
            for s in range(LOOP0):
                step(s, s)
            with act.Fori(0, LOOPN) as i:
                counter[0] = i
                for u in range(UNROLL):
                    step(UNROLL * i + (LOOP0 + u), LOOP0 + u)
            for s in range(LOOP0 + UNROLL * LOOPN, NS):
                step(s, s)
            out_y(NS - 2, NS - 2)
            out_y(NS - 1, NS - 1)
            for t in range(HALF, NT):
                inner_hi(t)

        @block.vector
        def _(dve):
            steps = [0]

            def then(ins):
                steps[0] += 1
                ins.then_inc(dve_step, 1)
                dve.wait_ge(dve_step, steps[0])

            def bn(t):
                then(nc.vector.bn_stats(stats[:, t, :], xs[:, t, :]))
                then(nc.vector.bn_aggr(meanvar[:, t, :], stats[:, t, :]))

            def var(a, b):
                nc.vector.tensor_scalar(vareps[:, a:b], meanvar[:, a:b, 1], EPS, None, ALU.add).then_inc(var_ready, 1)

            def lo_of(name, n, lo, raw, hi, part):
                dve.wait_ge(split_hi[name], n)
                nc.vector.tensor_tensor(lo, raw, hi.bitcast(F32), ALU.subtract).then_inc(split_lo[name + part], 1)

            def normalise(layer, h, js=range(HALF)):
                for j in js:
                    t = h * HALF + j
                    if t % 2 == 0:
                        dve.wait_ge(rstd_ready, layer * HALF + t // 2 + 1)
                    nc.vector.tensor_scalar(xn[:, t, :], xs[:, t, :], meanvar[:, t, 0:1], rstd[:, t:t + 1],
                                            ALU.subtract, ALU.mult).then_inc(xn_ready, 1)

            def xT_lo(m, h, js):
                for j in js:
                    dve.wait_ge(ring_hi, hi_count(m, j))
                    nc.vector.tensor_tensor(xT[h][:, 1, :, j * P:(j + 1) * P],
                                            bank[RING[m + j]][:].rearrange("p (c t) -> p c t", c=C),
                                            xT[h][:, 0, :, j * P:(j + 1) * P].bitcast(F32), ALU.subtract)\
                        .then_inc(ring_out, 1)

            def hi_count(m, j):
                return {0: 0, 4: 4, 12: 8, 20: 12}[m] + j + 1

            def softmax_shift(h):
                dve.wait_ge(score_done, h + 1)
                s = bank[6][:].rearrange("p (t k) -> p t k", t=HALF)
                mx = smax[:, h * HALF:(h + 1) * HALF]
                for b in range(2):
                    r = slice(b * SEQ, (b + 1) * SEQ)
                    then(nc.vector.tensor_reduce(mx[r, :], s[r, :, r], AX.X, ALU.max))
                for b in range(2):
                    r = slice(b * SEQ, (b + 1) * SEQ)
                    last = nc.vector.tensor_tensor(E[h][r, :, r], s[r, :, r],
                                                   mx[r, :].unsqueeze(2).to_broadcast([SEQ, HALF, SEQ]), ALU.subtract)
                    if b == 0:
                        last.then_inc(shift_half, 1)
                last.then_inc(shifted, 1)

            def softmax_sum(h):
                dve.wait_ge(exp_done, h + 1)
                dve.wait_ge(exp_half, h + 1)
                a, b = h * HALF, (h + 1) * HALF
                then(nc.vector.tensor_reduce(ssum[:, a:b], E[h], AX.X, ALU.add))
                then(nc.vector.reciprocal(rsum[:, a:b], ssum[:, a:b]))

            def residual(m, h, js):
                for j in js:
                    t = h * HALF + j
                    dve.wait_ge(ring_done, m + j + 1)
                    nc.vector.scalar_tensor_tensor(out=xs[:, t, :], in0=bank[RING[m + j]][:],
                                                   scalar=rsum[:, t:t + 1], in1=xs[:, t, :],
                                                   op0=ALU.mult, op1=ALU.add).then_inc(ring_out, 1)
                for j in js:
                    dve.wait_ge(ring_out, m + j + 1)
                    bn(h * HALF + j)
                var(h * HALF + js[0], h * HALF + js[0] + 2)

            def pair_mul(n):
                dve.wait_ge(pair_silu, n + 1)
                dve.wait_ge(up_done, n + 1)
                nc.vector.tensor_tensor(hsT[n // SC][:, n % SC, :], bank[2 * (n % 2) + 1][:], silu_s[n % 2][:], ALU.mult)\
                    .then_inc(pair_out, 1)

            def add_shared(t):
                dve.wait_ge(ring_done, 24 + t + 1)
                nc.vector.tensor_tensor(xs[:, t, :], bank[RING[24 + t]][:], xs[:, t, :], ALU.add).then_inc(ring_out, 1)

            nc.vector.memset(silu_s[0][:, 0:256], 1.0).then_inc(warm_ready, 1)

            for c in range(C):
                for w, raw, split in ((0, wk_raw, wkT), (1, ctx_raw[0], ctx0T)):
                    dve.wait_ge(split_hi["key"], 2 * c + w + 1)
                    nc.vector.tensor_tensor(split[:, 1, c], raw[:, c], split[:, 0, c].bitcast(F32), ALU.subtract)\
                        .then_inc(split_lo["key"], 1)
            for h in range(2):
                dve.wait_ge(ld[f"x{h}"], 16)
                for t in range(h * HALF, (h + 1) * HALF):
                    bn(t)
                    if t % 2:
                        var(t - 1, t + 1)
                if h == 0:
                    normalise(0, 0)
                    lo_of("ctx1", 2, ctx1T[:, 1, 2:4], ctx_raw[1][:, 2:4], ctx1T[:, 0, 2:4], "b")
                    xT_lo(0, 0, range(HALF))
            normalise(0, 1)
            xT_lo(4, 1, range(HALF))
            dve.wait_ge(const_step, 3)
            softmax_shift(0)
            softmax_sum(0)
            residual(8, 0, (0, 1))
            residual(8, 0, (2, 3))
            normalise(1, 0, (2, 3))
            xT_lo(12, 0, range(HALF))
            softmax_shift(1)
            softmax_sum(1)
            pair_mul(0)
            residual(16, 1, (0, 1))
            residual(16, 1, (2, 3))
            normalise(1, 1, (2, 3))
            pair_mul(1)
            xT_lo(20, 1, range(HALF))
            pair_mul(2)

            dve.wait_ge(logit_done, 2)
            dve.wait_ge(const_ready, 9)
            lg = bank[6][:, 0:2 * NT * NE].rearrange("p (t i e) -> p t i e", t=NT, i=2)

            def over_e(ap):
                return ap.unsqueeze(2).to_broadcast([P, NT, NE])

            then(nc.vector.tensor_copy(prob[:], lg[:, :, 1]))
            then(nc.vector.tensor_tensor(prob[:], lg[:, :, 0], prob[:], ALU.add))
            then(nc.vector.tensor_reduce(rmax[:], prob[:], AX.X, ALU.max))
            nc.vector.tensor_tensor(prob[:], prob[:], over_e(rmax[:]), ALU.subtract).then_inc(rshift, 1)
            dve.wait_ge(rexp, 1)
            then(nc.vector.tensor_reduce(psm[:], prob[:], AX.X, ALU.add))
            then(nc.vector.reciprocal(prs[:], psm[:]))
            then(nc.vector.tensor_tensor(prob[:], prob[:], over_e(prs[:]), ALU.mult))
            for t in range(NT):
                then(nc.vector.max(top[:, t, :], prob[:, t, :]))
            for t in range(NT):
                then(nc.vector.max_index(topi[:, t, :], top[:, t, :], prob[:, t, :]))
            then(nc.vector.tensor_copy(topf[:], topi[:, :, 0:TOPK]))
            it = iota_f[:, 0:NE].unsqueeze(1).to_broadcast([P, NT, NE])
            for k in range(TOPK):
                then(nc.vector.tensor_tensor(pick[k][:], it, over_e(topf[:, :, k]), ALU.is_equal))
            nc.vector.tensor_tensor(picked[:], pick[0][:], pick[1][:], ALU.add).then_inc(picked_ready, 1)
            then(nc.vector.tensor_tensor(wsum[:], top[:, :, 0], top[:, :, 1], ALU.add))
            then(nc.vector.reciprocal(wrec[:], wsum[:]))
            then(nc.vector.tensor_tensor(wtop[:], top[:, :, 0:TOPK], wrec[:].unsqueeze(2).to_broadcast([P, NT, TOPK]),
                                         ALU.mult))
            pair_mul(3)
            dve.wait_ge(count_done, 1)
            then(nc.vector.tensor_tensor(over[:], bank[6][:, 256:256 + NE].unsqueeze(2).to_broadcast([P, NE, 8]),
                                         steps128[:].unsqueeze(1).to_broadcast([P, NE, 8]), ALU.is_gt))
            then(nc.vector.tensor_reduce(ntile[:], over[:], AX.X, ALU.add))
            then(nc.vector.tensor_tensor(prod_e[:], lower_e[:], ntile[:].unsqueeze(1).to_broadcast([P, NE, NE]),
                                         ALU.mult))
            then(nc.vector.tensor_reduce(first[:], prod_e[:], AX.X, ALU.add))
            then(nc.vector.scalar_tensor_tensor(out=place[:], in0=first[:].unsqueeze(1).to_broadcast([P, NT, NE]),
                                                scalar=float(P),
                                                in1=bank[7][:, 0:NT * NE].rearrange("p (t e) -> p t e", t=NT),
                                                op0=ALU.mult, op1=ALU.add))
            for k in range(TOPK):
                then(nc.vector.tensor_tensor(placed[k][:], pick[k][:], place[:], ALU.mult))
            for k in range(TOPK):
                then(nc.vector.tensor_reduce(rows[:, :, k], placed[k][:], AX.X, ALU.add))
            then(nc.vector.tensor_copy(rows_i[:], rows[:]))
            nc.vector.tensor_copy(rows_u[:], rows[:]).then_inc(rows_ready, 1)
            then(nc.vector.tensor_scalar(slot_i[:], rows_i[:], 7, None, ALU.arith_shift_right))
            then(nc.vector.tensor_copy(slot_f[:], slot_i[:]))
            then(nc.vector.scalar_tensor_tensor(out=inrow[:], in0=slot_f[:], scalar=-float(P), in1=rows[:],
                                                op0=ALU.mult, op1=ALU.add))
            R = NT * TOPK
            sf = slot_f[:].rearrange("p t k -> p (t k)")
            ir = inrow[:].rearrange("p t k -> p (t k)")
            dve.wait_ge(xn_stored, 32)
            its = iota_f[:, 0:32].unsqueeze(1).to_broadcast([P, R, 32])
            sfs = sf.unsqueeze(2).to_broadcast([P, R, 32])
            then(nc.vector.tensor_tensor(slothot[:, :, 0, :], its, sfs, ALU.is_equal))
            nc.vector.tensor_tensor(slothot[:, :, 1, :].rearrange("p (t k) s -> p t k s", k=TOPK),
                                    slothot[:, :, 0, :].rearrange("p (t k) s -> p t k s", k=TOPK),
                                    tile_no[:].unsqueeze(2).unsqueeze(3).to_broadcast([P, NT, TOPK, 32]), ALU.mult)\
                .then_inc(slothot_ready, 1)
            dve.wait_ge(slothot_ready, 1)
            nc.vector.tensor_scalar(slothot[:, :, 0, :], slothot[:, :, 0, :], tile_row[:, 0:1], None, ALU.mult)\
                .then_inc(slothot_ready, 1)
            pair_mul(4)
            for n in range(R):
                nc.vector.tensor_scalar(rowhot[n][:], iota_f[:], ir[:, n:n + 1], None, ALU.is_equal)\
                    .then_inc(rowhot_ready, 1)
            then(nc.vector.tensor_tensor(last_e[:], first[0:1, :], ntile[0:1, :], ALU.add))
            nc.vector.tensor_tensor(past[:], last_e[:].unsqueeze(1).to_broadcast([1, 32, NE]),
                                    iota_f[0:1, 0:32].unsqueeze(2).to_broadcast([1, 32, NE]), ALU.is_le)\
                .then_inc(dve_step, 1)
            steps[0] += 1
            dve.wait_ge(map_done, 1)
            then(nc.vector.tensor_copy(src_tile[:], bank[7][:, 288:320]))
            nc.vector.scalar_tensor_tensor(out=src_rows[:], in0=src_tile[:], scalar=float(P), in1=bank[7][:, 256:288],
                                           op0=ALU.mult, op1=ALU.add).then_inc(src_ready, 1)
            then(nc.vector.tensor_reduce(slot_e[:], past[:], AX.X, ALU.add))
            nc.vector.tensor_scalar(slot_exp[:], slot_e[:], float(NE - 1), None, ALU.min).then_inc(exp_table, 1)
            pair_mul(5)
            pair_mul(6)

            def out_h(s, m):
                dve.wait_ge(h_turned, s + 1)
                ge(dve, y_done, s - 1)
                nc.vector.tensor_copy(hT[m % 2][:], bank[2 + m % 2][:, 0:P]).then_inc(hT_out, 1)

            def mul_h(s, m):
                dve.wait_ge(silu_done, s + 1)
                ge(dve, h_turned, s - 1)
                nc.vector.tensor_tensor(hh[m % 2][:], bank[m % 2][:, FE:2 * FE], sg[m % 2][:], ALU.mult)\
                    .then_inc(h_ready, 1)

            def weights_lo(s, m, e, a):
                dve.wait_ge(w_hi, s + 1)
                nc.vector.tensor_tensor(wsp[m % 2][:, 1, a:a + 2, :], raw_gu(e, a),
                                        wsp[m % 2][:, 0, a:a + 2, :].bitcast(F32), ALU.subtract).then_inc(w_lo, 1)

            def tokens_lo(s, m):
                dve.wait_ge(gT_hi, s + 1)
                nc.vector.tensor_tensor(gT[m % 2][:, 1], bank[4 + m % 2][:].rearrange("p (c t) -> p c t", c=C),
                                        gT[m % 2][:, 0].bitcast(F32), ALU.subtract).then_inc(gT_out, 1)

            def step(s, m):
                more = not (isinstance(s, int) and s + 1 >= NS)
                if more:
                    e = expert_of(dve, s + 1)
                    weights_lo(s + 1, m + 1, e, 0)
                if m:
                    out_h(s - 1, m - 1)
                if more:
                    tokens_lo(s + 1, m + 1)
                mul_h(s, m)
                if more:
                    weights_lo(s + 1, m + 1, e, 2)

            dve.wait_ge(exp_table, 1)
            e = expert_of(dve, 0)
            weights_lo(0, 0, e, 0)
            tokens_lo(0, 0)
            weights_lo(0, 0, e, 2)
            pair_mul(7)
            slot_steps(dve, step)
            out_h(NS - 1, NS - 1)

            def combine(t):
                for k in range(TOPK):
                    n = t * TOPK + k
                    dve.wait_ge(back[n % NB], 16 * (n // NB + 1))
                    if k:
                        dve.wait_ge(back_used, n)
                    last = nc.vector.scalar_tensor_tensor(out=xs[:, t, :], in0=gback[n % NB][:],
                                                          scalar=wtop[:, t, k:k + 1], in1=xs[:, t, :],
                                                          op0=ALU.mult, op1=ALU.add)
                    last.then_inc(back_used, 1)

            def inner_lo(t):
                dve.wait_ge(hs_hi, t + 1)
                r = slice(t % HALF * P, (t % HALF + 1) * P)
                nc.vector.tensor_tensor(hsT_lo[1][:, :, r], hsT[1][:, :, r], hsT_hi[t][:].bitcast(F32), ALU.subtract)\
                    .then_inc(hs_lo[1], 1)

            inner_lo(4)
            add_shared(0)
            inner_lo(5)
            add_shared(1)
            inner_lo(6)
            inner_lo(7)
            add_shared(2)
            shared_before = {2: 3, 3: 4, 4: 5, 5: 6, 6: 7}
            for t in range(NT):
                if t in shared_before:
                    add_shared(shared_before[t])
                dve.wait_ge(ring_out, 24 + t + 1)
                combine(t)


_OUT = ((16, 64, 512), 'float32')


def kernel(x, ctx_4096, L0_xattn_Wq, L0_xattn_bq, L0_xattn_Wk, L0_xattn_bk, L0_ffn_gate_w, L0_ffn_w_gate_up,
           L0_ffn_w_down, L0_ffn_shared_w_gate_up, L0_ffn_shared_w_down):
    import numpy as np
    import concourse.bacc as bacc
    from concourse.bass_utils import run_bass_kernel_spmd

    def feature_chunks(a):
        a = np.asarray(a)
        a = a.reshape(a.shape[:-1] + (a.shape[-1] // 128, 128))
        return np.ascontiguousarray(np.moveaxis(a, (-1, -2), (0, 1)))

    def token_tiles(a):
        a = np.asarray(a).reshape(8, 128, 512)
        return np.ascontiguousarray(a.transpose(1, 0, 2))

    gu = np.asarray(L0_ffn_w_gate_up)
    arrays = {
        "x": token_tiles(x),
        "ctx_t": feature_chunks(np.asarray(ctx_4096).reshape(1024, 512)),
        "ctx_n": token_tiles(ctx_4096),
        "wq_t": feature_chunks(L0_xattn_Wq),
        "wk_t": feature_chunks(L0_xattn_Wk),
        "bq": feature_chunks(L0_xattn_bq),
        "bk": feature_chunks(L0_xattn_bk),
        "gate_t": feature_chunks(L0_ffn_gate_w),
        "moe_gu_t": np.ascontiguousarray(feature_chunks(gu).transpose(0, 2, 1, 3)),
        "moe_dn_t": np.ascontiguousarray(np.asarray(L0_ffn_w_down).transpose(2, 0, 1)),
        "sh_gu_t": np.ascontiguousarray(feature_chunks(L0_ffn_shared_w_gate_up).reshape(128, 4, 2, 4, 128)
                                        .transpose(0, 3, 2, 1, 4)),
        "sh_dn_t": feature_chunks(L0_ffn_shared_w_down),
    }
    nc = bacc.Bacc("TRN2", target_bir_lowering=False, num_devices=1)
    args = [nc.dram_tensor(n, a.shape, mybir.dt.from_np(a.dtype), kind="ExternalInput").ap()
            for n, a in arrays.items()]
    out = nc.dram_tensor("out", (128, 8, 512), F32, kind="ExternalOutput").ap()
    xattn_moe(nc, *args, out)
    r = run_bass_kernel_spmd(nc, [arrays], core_ids=[0])
    got = r.results[0]["out"]
    return np.ascontiguousarray(got.transpose(1, 0, 2)).reshape(_OUT[0])
```
